# Optimizing a Trainium2 kernel written in Bass

```python
import numpy as np
import jax
import jax.numpy as jnp

def _softmax(x, axis=-1):
    return jax.nn.softmax(x, axis=axis)

def _gelu(x):
    return jax.nn.gelu(x, approximate=True)

def _silu(x):
    return jax.nn.silu(x)

def _sigmoid(x):
    return jax.nn.sigmoid(x)

def _layernorm(x, axis=-1, eps=1e-05):
    m = jnp.mean(x, axis=axis, keepdims=True)
    v = jnp.var(x, axis=axis, keepdims=True)
    return (x - m) / jnp.sqrt(v + eps)

def _scatter_add(tgt, idx, src, axis=0):
    return tgt.at[idx].add(src)

def _segment_sum(src, seg, n):
    return jax.ops.segment_sum(src, seg, n)
kernel_name = 'mk_seq_postln_d1_jaxref_r8_6f9bcb'

def setup_inputs(seed: int=0):
    np.random.seed(seed)
    _w = jnp.asarray

    def _L0_attn_setup():
        import jax, jax.numpy as jnp
        import numpy as np
        from jax import lax
        B_SZ, L, D_INNER, D_STATE, DT_RANK = (2, 256, 256, 16, 64)
        key = jax.random.key(seed)
        k = jax.random.split(key, 6)
        x = jax.random.normal(k[0], (B_SZ, L, D_INNER), dtype=jnp.float32)
        A = jnp.tile(jnp.arange(1, D_STATE + 1, dtype=jnp.float32)[None, :], (D_INNER, 1))
        A_log = jnp.log(A)
        D = jnp.ones((D_INNER,), dtype=jnp.float32)
        dt_init_std = DT_RANK ** (-0.5)
        W_x = jax.random.normal(k[1], (DT_RANK + 2 * D_STATE, D_INNER), dtype=jnp.float32) * D_INNER ** (-0.5)
        W_dt = jax.random.uniform(k[2], (D_INNER, DT_RANK), dtype=jnp.float32, minval=-dt_init_std, maxval=dt_init_std)
        dt = jnp.exp(jax.random.uniform(k[3], (D_INNER,), dtype=jnp.float32) * (np.log(0.1) - np.log(0.001)) + np.log(0.001))
        dt = jnp.clip(dt, 0.001, None)
        b_dt = dt + jnp.log(-jnp.expm1(-dt))
        return {'x': x, 'A_log': A_log, 'D': D, 'W_x': W_x, 'W_dt': W_dt, 'b_dt': b_dt}
    _L0_attn_in = _L0_attn_setup()

    def _L0_ffn_setup():
        import jax, jax.numpy as jnp
        import numpy as np
        B, S, H = (4, 256, 256)
        INTER = 512
        E = 8
        TOPK = 2
        SHARED_I = INTER * 2

        def moe_forward(hidden_states, router_w, w1, w2, w_gate, w_up, w_down):
            b, s, h = hidden_states.shape
            x = hidden_states.reshape(-1, h)
            T = x.shape[0]
            logits = x @ router_w
            top_logits, top_indices = jax.lax.top_k(logits, TOPK)
            scores = jax.nn.softmax(top_logits, axis=-1)
            flat_idx = top_indices.reshape(-1)
            sorted_pos = jnp.argsort(flat_idx, stable=True)
            permuted = x[sorted_pos // TOPK]
            expert_ids = flat_idx[sorted_pos]
            out = jnp.zeros((T * TOPK, h), x.dtype)
            for e in range(E):
                mask = (expert_ids == e)[:, None]
                f1 = permuted * mask @ w1[e]
                g, u = jnp.split(f1, 2, axis=-1)
                act = jax.nn.silu(g) * u
                out = out + jnp.where(mask, act @ w2[e], 0.0)
            unperm = jnp.zeros_like(out).at[sorted_pos].set(out)
            combined = (unperm.reshape(T, TOPK, h) * scores[..., None]).sum(axis=1)
            shared = jax.nn.silu(x @ w_gate) * (x @ w_up) @ w_down
            return (combined + shared).reshape(b, s, h)
        key = jax.random.key(seed)
        ks = jax.random.split(key, 7)
        s = 0.02
        return {'hidden_states': jax.random.normal(ks[0], (B, S, H), jnp.float32), 'router_w': jax.random.normal(ks[1], (H, E), jnp.float32) * s, 'w1': jax.random.normal(ks[2], (E, H, 2 * INTER), jnp.float32) * s, 'w2': jax.random.normal(ks[3], (E, INTER, H), jnp.float32) * s, 'w_gate': jax.random.normal(ks[4], (H, SHARED_I), jnp.float32) * s, 'w_up': jax.random.normal(ks[5], (H, SHARED_I), jnp.float32) * s, 'w_down': jax.random.normal(ks[6], (SHARED_I, H), jnp.float32) * s}
    _L0_ffn_in = _L0_ffn_setup()
    _d = {'L0_attn_x': _L0_attn_in['x'], 'L0_attn_A_log': _L0_attn_in['A_log'], 'L0_attn_D': _L0_attn_in['D'], 'L0_attn_W_x': _L0_attn_in['W_x'], 'L0_attn_W_dt': _L0_attn_in['W_dt'], 'L0_attn_b_dt': _L0_attn_in['b_dt'], 'L0_ffn_router_w': _L0_ffn_in['router_w'], 'L0_ffn_w1': _L0_ffn_in['w1'], 'L0_ffn_w2': _L0_ffn_in['w2'], 'L0_ffn_w_gate': _L0_ffn_in['w_gate'], 'L0_ffn_w_up': _L0_ffn_in['w_up'], 'L0_ffn_w_down': _L0_ffn_in['w_down']}
    _x0 = _d['L0_attn_x']
    _d['L0_attn_x'] = jax.random.normal(jax.random.fold_in(jax.random.key(seed), 1), (4, 512, 256), dtype=_x0.dtype)
    del _x0
    return _d

def reference(L0_attn_x, L0_attn_A_log, L0_attn_D, L0_attn_W_x, L0_attn_W_dt, L0_attn_b_dt, L0_ffn_router_w, L0_ffn_w1, L0_ffn_w2, L0_ffn_w_gate, L0_ffn_w_up, L0_ffn_w_down):

    def _L0_attn_ref(x, A_log, D, W_x, W_dt, b_dt):
        import jax, jax.numpy as jnp
        import numpy as np
        from jax import lax
        B_SZ, L, D_INNER, D_STATE, DT_RANK = (2, 256, 256, 16, 64)
        A = -jnp.exp(A_log)
        xp = jnp.einsum('bld,pd->blp', x, W_x)
        delta_p = xp[..., :DT_RANK]
        B_proj = xp[..., DT_RANK:DT_RANK + D_STATE]
        C_proj = xp[..., DT_RANK + D_STATE:]
        delta = jax.nn.softplus(jnp.einsum('blr,dr->bld', delta_p, W_dt) + b_dt)
        A_bar = jnp.exp(jnp.einsum('bld,dn->bldn', delta, A))
        Bx = jnp.einsum('bld,bln->bldn', delta, B_proj) * x[..., None]

        def step(h, inp):
            Ab_t, bx_t, c_t = inp
            h = Ab_t * h + bx_t
            y_t = jnp.einsum('bdn,bn->bd', h, c_t)
            return (h, y_t)
        h0 = jnp.zeros((x.shape[0], D_INNER, D_STATE), dtype=x.dtype)
        _, ys = lax.scan(step, h0, (A_bar.transpose(1, 0, 2, 3), Bx.transpose(1, 0, 2, 3), C_proj.transpose(1, 0, 2)))
        y = ys.transpose(1, 0, 2)
        return y + x * D

    def _L0_ffn_ref(hidden_states, router_w, w1, w2, w_gate, w_up, w_down):
        import jax, jax.numpy as jnp
        import numpy as np
        B, S, H = (4, 256, 256)
        INTER = 512
        E = 8
        TOPK = 2
        SHARED_I = INTER * 2

        def moe_forward(hidden_states, router_w, w1, w2, w_gate, w_up, w_down):
            b, s, h = hidden_states.shape
            x = hidden_states.reshape(-1, h)
            T = x.shape[0]
            logits = x @ router_w
            top_logits, top_indices = jax.lax.top_k(logits, TOPK)
            scores = jax.nn.softmax(top_logits, axis=-1)
            flat_idx = top_indices.reshape(-1)
            sorted_pos = jnp.argsort(flat_idx, stable=True)
            permuted = x[sorted_pos // TOPK]
            expert_ids = flat_idx[sorted_pos]
            out = jnp.zeros((T * TOPK, h), x.dtype)
            for e in range(E):
                mask = (expert_ids == e)[:, None]
                f1 = permuted * mask @ w1[e]
                g, u = jnp.split(f1, 2, axis=-1)
                act = jax.nn.silu(g) * u
                out = out + jnp.where(mask, act @ w2[e], 0.0)
            unperm = jnp.zeros_like(out).at[sorted_pos].set(out)
            combined = (unperm.reshape(T, TOPK, h) * scores[..., None]).sum(axis=1)
            shared = jax.nn.silu(x @ w_gate) * (x @ w_up) @ w_down
            return (combined + shared).reshape(b, s, h)
        return moe_forward(hidden_states, router_w, w1, w2, w_gate, w_up, w_down)
    x = L0_attn_x
    x = _layernorm(x + _L0_attn_ref(x, L0_attn_A_log, L0_attn_D, L0_attn_W_x, L0_attn_W_dt, L0_attn_b_dt), axis=-1)
    x = _layernorm(x + _L0_ffn_ref(x, L0_ffn_router_w, L0_ffn_w1, L0_ffn_w2, L0_ffn_w_gate, L0_ffn_w_up, L0_ffn_w_down), axis=-1)
    return x

_drawn_inputs = setup_inputs


def setup_inputs(seed=0):
    import zlib

    import numpy as np

    out = dict(_drawn_inputs(seed))
    spreads = {'L0_attn_D': (1.0, 0.2)}
    factors = {'L0_ffn_router_w': 3.848, 'L0_ffn_w1': 3.322, 'L0_ffn_w2': 3.325}
    for name, (base, spread) in spreads.items():
        noise = np.random.default_rng([zlib.crc32(name.encode()), seed]).standard_normal(out[name].shape)
        drawn = base * np.exp(spread * noise) if base else spread * noise
        out[name] = jnp.asarray(drawn.astype(out[name].dtype))
    for name, factor in factors.items():
        out[name] = (out[name] * factor).astype(out[name].dtype)
    return out
```

```python
from contextlib import ExitStack

import numpy as np
import concourse.bass as bass
from concourse import mybir

P = 128
NB = 4
L = 512
T = NB * L
D = 256
DT = D // P
NS = 16
GC = P // NS
NG = D // GC
NQ = NG // 4
R = 64
TT = L // P
E = 8
INTER = 512
SI = 1024
NI = SI // P
NBLK = (2 * T) // P + E - 1
REGION = T
NLIST = E * REGION + P
TRASH = T
EPS = 1e-5

F32 = mybir.dt.float32
F32R = mybir.dt.float32r
BF16 = mybir.dt.bfloat16
I32 = mybir.dt.int32
ACT = mybir.ActivationFunctionType
ALU = mybir.AluOpType
AX = mybir.AxisListType.X
ds = bass.ds

PREP = ["dp", "z0", "z1", "B", "C"]
POST = (["turn0", "turn1", "back0", "back1", "logits", "g0", "u0", "g1", "u1", "ranks"]
        + [f"{w}{i}" for i in range(2, NI) for w in "gu"] + ["down0", "down1"])
BANK = {n: k % 3 for k, n in enumerate(PREP + POST)}


PREP_AT = {0: ["dp"], 2: ["z0", "z1"], 4: ["B"], 5: ["C"]}
POST_AT = {7: ["turn0"], 8: ["turn1"], 11: ["back0"], 12: ["back1"], 15: ["logits", "g0"], 16: ["u0"], 17: ["g1"],
           18: ["u1"], 19: ["ranks"], 20: ["g2", "u2"], 21: ["g3"], 22: ["u3"], 23: ["g4", "u4"], 24: ["g5"],
           25: ["u5"], 26: ["g6"], 27: ["u6"], 28: ["g7"], 29: ["u7"], 30: ["down0"], 31: ["down1"]}
PREP_ACT = {0: ["dp"], 3: ["z0", "z1"], 4: ["log"], 5: ["B"], 6: ["C"], 9: ["hi0"], 10: ["hi1"]}
POST_ACT = {9: ["turn0"], 10: ["turn1"], 12: ["back0"], 13: ["back1"], 16: ["g0"], 18: ["g1"], 19: ["ex"],
            21: ["g2"], 22: ["g3"], 24: ["g4"], 25: ["g5"], 27: ["g6"], 29: ["g7"]}
PREP_DVE = {7: ["delta"], 8: ["dx"], 11: ["lo0"], 12: ["lo1"]}
POST_DVE = {8: ["turn0"], 9: ["turn1"], 13: ["back0"], 14: ["back1"], 16: ["logits"], 17: ["g0", "u0"],
            19: ["g1", "u1"], 20: ["ex", "ranks"], 21: ["g2", "u2"], 22: ["g3"], 23: ["u3"], 24: ["g4", "u4"],
            25: ["g5"], 26: ["u5"], 27: ["g6"], 28: ["u6"], 29: ["g7", "u7"], 31: ["down0", "down1"]}
POST_POOL = {9: ["turn0"], 10: ["turn1"], 22: ["scatter"], 26: ["landed"]}
Y1_AT, Y0_AT = 5, 21
RT_STEPS = 29
SETUP_ACT, SETUP_DVE = 6, 8


def uses(stage, m, name):
    k = BANK[name]
    p = sum(BANK[n] == k for n in PREP)
    q = sum(BANK[n] == k for n in POST)
    if stage == "prepared":
        names, before = PREP, m * p + (q if isinstance(m, int) and m == NB - 1 else 0)
    elif stage == "prep":
        names, before = PREP, m * p + ((m - 2) * q if not isinstance(m, int) or m > 2 else 0)
    else:
        names = POST
        before = m * q + (4 * p if isinstance(m, int) and m >= 2 else (m + 3) * p)
    return before + sum(BANK[n] == k for n in names[:names.index(name) + 1])


PACK = [("wp", DT * R), ("wbc", 2 * DT * P), ("bdt", DT), ("dpar", DT), ("alog", NG), ("ysel", 4 * 32),
        ("ident", P), ("lower", 2 * P), ("rw", DT * E), ("rev", E), ("region", E), ("expert", E), ("block", NBLK)]
COL = {}
for _name, _n in PACK:
    COL[_name] = (sum(n for _, n in COL.values()) if COL else 0, _n)
NPACK = sum(n for _, n in PACK)


def program(nc, A, out):
    xn_d = nc.dram_tensor("xn_rows", [T + P, D], F32).ap()
    acc_d = nc.dram_tensor("acc_rows", [T + P, D], F32).ap()
    list_d = nc.dram_tensor("slot_list", [NLIST, 2], I32).ap()

    with ExitStack() as ctx:
        top = [(nc.sbuf_base + 63) // 64 * 64]

        def at(name, shape, dt=F32, offset=None):
            size = int(np.prod(shape[1:])) * (2 if dt == BF16 else 4)
            if offset is None:
                offset = top[0]
                top[0] += (size + 31) // 32 * 32
            return nc.alloc_sbuf_tensor_at(name, shape, dt, offset=offset)

        def sem(name):
            return ctx.enter_context(nc.semaphore(name))

        pk = at("pack", [P, NPACK])

        def col(name, rows=P):
            o, n = COL[name]
            return pk[0:rows, o:o + n]

        ident = col("ident")
        rev, region = col("rev"), col("region")
        lower = at("lower", [P, 2, P], BF16)
        tok = at("tok", [P, T // P], I32)
        bn = at("bn", [P, TT, 6])
        mv = at("mv", [P, TT, 2])
        ve = at("ve", [P, TT])
        mhalf = at("mhalf", [P, TT])
        rstd = at("rstd", [P, TT])
        nbias = at("nbias", [P, TT])
        offs = at("offs", [P, TT + 1, E])
        lst = at("lst", [P, 4, 2], I32)
        lg = at("lg", [P, TT, E])
        lg2 = at("lg2", [P, TT, E])
        eq = at("eq", [P, 2, TT, E])
        key = at("key", [P, 2, TT, E])
        oh = at("oh", [P, 2, TT, E])
        oh_b = at("oh_b", [P, TT, E], BF16)
        rk = at("rk", [P, TT, E])
        rk2 = at("rk2", [P, TT, E])
        pr = at("pr", [P, 2, TT, E])
        mx = at("mx", [P, 2, TT])
        kk = at("kk", [P, 2, TT])
        gap = at("gap", [P, TT])
        ex = at("ex", [P, TT])
        den = at("den", [P, TT])
        sc = at("sc", [P, 2, TT])
        posf = at("posf", [P, 2, TT])
        pos = at("pos", [P, 2, TT], I32)
        ent = at("ent", [P, 2, TT, 2], I32)
        rhi = at("rhi", [P, DT, E], F32R)
        rlo = at("rlo", [P, DT, E], F32R)
        cnt = at("cnt", [1, 5, E])
        cnti = at("cnti", [1, 2, E], I32)
        btw = at("btw", [1, NBLK, E])
        btc = at("btc", [1, 8, NBLK])
        info = at("info", [1, 2, NBLK], I32)
        rT = at("rT", [P, DT, L])
        xn4 = at("xn4", [P, TT, D])
        xhi = at("xhi", [P, DT, L], F32R)
        xlo = at("xlo", [P, DT, L], F32R)
        th_offset = top[0]
        th = at("th", [P, 2, L])
        act_offset = top[0]
        act = at("act", [P, NI, L])
        wg_hi = at("wg_hi", [P, 2, DT, SI], F32R)
        wg_lo = at("wg_lo", [P, 2, DT, SI], F32R)
        wd = at("wd", [P, NI, D])
        sel_raw = at("sel_raw", [P, 8, P], F32, th_offset)
        wg_raw = at("wg_raw", [P, 2, DT, SI], F32, act_offset)
        epoch = top[0]
        xT = at("xT", [P, DT, T])
        hl = [at("hl_delta", [P, 2, 4, L], F32R), at("hl_dx", [P, 2, 4, L], F32R)]
        bc = at("bc", [P, 2, 2, L])
        rel = at("rel", [P, DT, L])
        lnt = at("lnt", [P, DT, L])
        hi = [at("hi_delta", [P, DT, L], F32R), at("hi_dx", [P, DT, L], F32R)]
        lo = [at("lo_delta", [P, DT, L], F32R), at("lo_dx", [P, DT, L], F32R)]
        dps = at("dps", [R, L])
        bx = at("bx", [P, 2, L])
        h = at("h", [P, 4, L])
        hc = at("hc", [P, 8, L])
        sel = at("sel", [P, 8, P], F32R)
        wdt = at("wdt", [R, D])
        aneg = at("aneg", [P, NG])
        dp1 = at("dp1", [P, DT])
        end_scan = top[0]
        assert end_scan <= nc.sbuf_usable_end, (end_scan, nc.sbuf_usable_end)
        top[0] = epoch
        w1 = at("w1", [P, E, DT, 2 * INTER])
        w2 = at("w2", [P, E, INTER // P, D])
        xb = at("xb", [P, 4, D])
        xbT = at("xbT", [P, 2, DT, P])
        sg = at("sg", [P, 2, INTER])
        ab = at("ab", [P, 2, INTER])
        aT = at("aT", [P, 2, INTER])
        ob = at("ob", [P, 2, D])
        fin = at("fin", [P, 2, TT, D], F32, epoch)
        fin_o = at("fin_o", [P, 2, TT, D], F32, epoch + 2 * TT * D * 4)
        assert top[0] <= nc.sbuf_usable_end
        bank = [ctx.enter_context(nc.psum_tensor(f"bank{k}", [P, L], F32)) for k in range(8)]
        da, dxp, yp, work = bank[0:2], bank[2:4], bank[4], bank[5:8]
        gate_p, up_p = [bank[0], bank[2]], [bank[1], bank[3]]
        xt_p, at_p, out_p = bank[4], bank[5], bank[6:8]

        packed = sem("packed")
        x_in = sem("x_in")
        sel_in = sem("sel_in")
        wdt_in = sem("wdt_in")
        shared_in = sem("shared_in")
        down_in = sem("down_in")
        tok_in = sem("tok_in")
        const_ready = sem("const_ready")
        dconst = sem("dconst")
        full = [sem(f"work_full{k}") for k in range(3)]
        drained = [sem(f"work_drained{k}") for k in range(3)]
        z_exp = sem("z_exp")
        z_log = sem("z_log")
        delta_ready = sem("delta_ready")
        dx_ready = sem("dx_ready")
        hi_ready = sem("hi_ready")
        lo_ready = sem("lo_ready")
        moved = sem("moved")
        decay_in = sem("decay_in")
        drive_in = sem("drive_in")
        decay_ready = sem("decay_ready")
        bx_ready = sem("bx_ready")
        scanned = sem("scanned")
        hc_ready = sem("hc_ready")
        y_quads = sem("y_quads")
        y_taken = sem("y_taken")
        stats = sem("stats")
        bn_step = sem("bn_step")
        rs_step = sem("rs_step")
        rstd_ready = sem("rstd_ready")
        xn_out = sem("xn_out")
        xhi_ready = sem("xhi_ready")
        picked = sem("picked")
        ex_ready = sem("ex_ready")
        rt_step = sem("rt_step")
        ent_ready = sem("ent_ready")
        scattered = sem("scattered")
        th_ready = sem("th_ready")
        sums_out = sem("sums_out")
        info_ready = sem("info_ready")
        w_in = sem("w_in")
        list_in = [sem(f"list_in{k}") for k in range(4)]
        rows_in = [sem(f"rows_in{k}") for k in range(4)]
        xt_full = sem("xt_full")
        xbT_ready = sem("xbT_ready")
        gate_full = sem("gate_full")
        up_full = sem("up_full")
        sg_ready = sem("sg_ready")
        ab_ready = sem("ab_ready")
        at_full = sem("at_full")
        aT_ready = sem("aT_ready")
        out_full = sem("out_full")
        ob_ready = sem("ob_ready")
        added = sem("added")
        fin_in = [sem(f"fin_in{k}") for k in range(2)]
        fin_rstd = sem("fin_rstd")
        padded = sem("padded")
        passed = sem("passed")
        info_step = sem("info_step")
        fin_ready = sem("fin_ready")
        fin_out = sem("fin_out")
        block = ctx.enter_context(nc.Block())

        hl_flat = [t[:, :, :, :].rearrange("p a c l -> p (a c l)") for t in hl]
        bc_flat = bc[:, :, :, :].rearrange("p a s l -> p (a s l)")

        def geometry(n):
            dt, s = divmod(n, NG // DT)
            q, k = s % 4, s // 4
            return dt, q, k, 2 * dt + q // 2, (q % 2) * 4 + k

        def parity(eng, m):
            return m % 2 if isinstance(m, int) else eng.snap(m % 2)

        def filled(eng, stage, m, name):
            eng.wait_ge(full[BANK[name]], uses(stage, m, name))
            return work[BANK[name]]

        def drain_of(eng, stage, m, name):
            eng.wait_ge(drained[BANK[name]], uses(stage, m, name))

        def alone(eng):
            eng.sem_inc(passed, 1)

        def blocks(eng, step):
            for c in range(4):
                step(0, c)
            with eng.Fori(0, NBLK // 4 - 1) as i:
                for c in range(4, 8):
                    step(i, c)
            for c in range(NBLK // 4 * 4, NBLK):
                step(0, c)

        def start(eng, m):
            return m * L if isinstance(m, int) else eng.snap(m * L)

        @block.tensor
        def _(pe):
            def fill(stage, m, name):
                u = uses(stage, m, name)
                if not (isinstance(u, int) and u == 1):
                    pe.wait_ge(drained[BANK[name]], u - 1)
                return work[BANK[name]]

            def prep(m, name):
                w = None
                tok0 = start(pe, m)
                if name == "dp":
                    if isinstance(m, int):
                        pe.wait_ge(x_in, 16 * (m + 1))
                    w = fill("prep", m, name)
                    for k in range(DT):
                        mm = nc.tensor.matmul(w[0:R, :], col("wp")[:, k * R:(k + 1) * R], xT[:, k, ds(tok0, L)],
                                              start=(k == 0), stop=(k == DT - 1))
                elif name in ("z0", "z1"):
                    w = fill("prep", m, name)
                    dt = int(name[1])
                    if dt == 0:
                        drain_of(pe, "prep", m, "dp")
                    mm = nc.tensor.matmul(w[:, :], wdt[:, dt * P:(dt + 1) * P], dps[:, :], start=True, stop=True)
                else:
                    w = fill("prep", m, name)
                    o = "BC".index(name) * DT * P
                    for k in range(DT):
                        mm = nc.tensor.matmul(w[:, :], col("wbc")[:, o + k * P:o + (k + 1) * P],
                                              xT[:, k, ds(tok0, L)], start=(k == 0), stop=(k == DT - 1))
                mm.then_inc(full[BANK[name]], 1)

            def expand(b, n, par):
                dt, q, k, c, j = geometry(n)
                if not (isinstance(b, int) and NG * b + n < 2):
                    pe.wait_ge(scanned, NG * b + n - 1)
                nc.tensor.matmul(da[n % 2][:, :], sel[:, j, :], hl_flat[0][:, ds(par * 4 * L + c * L, L)],
                                 start=True, stop=True).then_inc(decay_in, 1)
                nc.tensor.matmul(dxp[n % 2][:, :], sel[:, j, :], hl_flat[1][:, ds(par * 4 * L + c * L, L)],
                                 start=True, stop=True).then_inc(drive_in, 1)

            def sum_quad(b, k):
                pe.wait_ge(hc_ready, NG * b + 4 * k + 4)
                if k % 4 == 0 and not (isinstance(b, int) and b == 0 and k == 0):
                    pe.wait_ge(y_taken, DT * b + k // 4)
                for q in range(4):
                    mm = nc.tensor.matmul(yp[32 * q:32 * q + 32, :], col("ysel")[:, (k % 4) * 32:(k % 4) * 32 + 32],
                                          hc[:, (4 * k + q) % 8, :], start=(k % 4 == 0), stop=(k % 4 == 3))
                mm.then_inc(y_quads, 1)

            def post(m, name):
                if name in ("turn0", "turn1"):
                    i = int(name[4])
                    if i == 0:
                        pe.wait_ge(y_taken, DT * (m + 1))
                    w = fill("post", m, name)
                    for t in range(2):
                        for dt in range(DT):
                            mm = nc.tensor.transpose(w[:, t * D + dt * P:t * D + (dt + 1) * P],
                                                     rT[:, dt, (2 * i + t) * P:(2 * i + t + 1) * P], ident)
                    mm.then_inc(full[BANK[name]], 1)
                elif name in ("back0", "back1"):
                    dt = int(name[4])
                    if dt == 0:
                        drain_of(pe, "post", m, "turn1")
                    w = fill("post", m, name)
                    for t in range(TT):
                        mm = nc.tensor.transpose(w[:, t * P:(t + 1) * P], xn4[:, t, dt * P:(dt + 1) * P], ident)
                    mm.then_inc(full[BANK[name]], 1)
                elif name == "logits":
                    drain_of(pe, "post", m, "back1")
                    w = fill("post", m, name)
                    for t in range(TT):
                        terms = [(x, r, k) for x in (xhi, xlo) for r in (rhi, rlo) for k in range(DT)]
                        for i, (x, r, k) in enumerate(terms):
                            mm = nc.tensor.matmul(w[:, t * E:(t + 1) * E], x[:, k, t * P:(t + 1) * P], r[:, k, :],
                                                  start=(i == 0), stop=(i == len(terms) - 1))
                    mm.then_inc(full[BANK[name]], 1)
                elif name == "ranks":
                    pe.wait_ge(picked, m + 1)
                    w = fill("post", m, name)
                    nc.tensor.matmul(w[:, 0:TT * E], lower[:, 0, :], oh_b[:, :, :].rearrange("p t e -> p (t e)"),
                                     start=True, stop=True)
                    nc.tensor.matmul(w[:, TT * E:2 * TT * E], lower[:, 1, :],
                                     oh_b[:, :, :].rearrange("p t e -> p (t e)"),
                                     start=True, stop=True).then_inc(full[BANK[name]], 1)
                elif name[0] in "gu":
                    i, side = int(name[1:]), "gu".index(name[0])
                    w = fill("post", m, name)
                    terms = [(a, x, k) for a, x in ((wg_hi, xhi), (wg_hi, xlo), (wg_lo, xhi)) for k in range(DT)]
                    for t, (a, x, k) in enumerate(terms):
                        mm = nc.tensor.matmul(w[:, :], a[:, side, k, i * P:(i + 1) * P], x[:, k, :],
                                              start=(t == 0), stop=(t == len(terms) - 1))
                    mm.then_inc(full[BANK[name]], 1)
                else:
                    i = int(name[4])
                    drain_of(pe, "post", m, "u7")
                    w = fill("post", m, name)
                    for t in range(2):
                        for k in range(NI):
                            mm = nc.tensor.matmul(w[:, t * D:(t + 1) * D],
                                                  act[:, k, (2 * i + t) * P:(2 * i + t + 1) * P], wd[:, k, :],
                                                  start=(k == 0), stop=(k == NI - 1))
                    mm.then_inc(full[BANK[name]], 1)

            def batch(b, with_prep, with_post):
                par = parity(pe, b)
                pe.wait_ge(moved, 128 * (b + 1))
                for n in range(NG):
                    expand(b, n, par)
                    if n % 4 == 3:
                        if n > 3:
                            sum_quad(b, n // 4 - 1)
                        elif with_post:
                            sum_quad(b - 1, NQ - 1)
                    if with_prep and n in PREP_AT:
                        for name in PREP_AT[n]:
                            prep(b + 1, name)
                    if with_post and n in POST_AT:
                        for name in POST_AT[n]:
                            post(b - 1, name)

            pe.wait_ge(packed, 16)
            pe.wait_ge(wdt_in, 16)
            for name in PREP:
                prep(0, name)
            pe.wait_ge(const_ready, SETUP_ACT)
            pe.wait_ge(dconst, SETUP_DVE)
            pe.wait_ge(down_in, 16)
            batch(0, True, False)
            with pe.Fori(1, NB - 1) as b:
                batch(b, True, True)
            batch(NB - 1, False, True)
            sum_quad(NB - 1, NQ - 1)
            for name in POST:
                post(NB - 1, name)

            w1_flat = w1[:, :, :, :].rearrange("p e k n -> p (e k n)")
            w2_flat = w2[:, :, :, :].rearrange("p e k n -> p (e k n)")

            def turn_rows(i, c):
                pe.wait_ge(rows_in[c % 4], 16 * i + 16 * (c // 4 + 1))
                if c >= 1:
                    pe.wait_ge(xbT_ready, 4 * i + c)
                for dt in range(DT):
                    mm = nc.tensor.transpose(xt_p[:, dt * P:(dt + 1) * P], xb[:, c % 4, dt * P:(dt + 1) * P], ident)
                mm.then_inc(xt_full, 1)

            def up(i, c):
                expert = pe.value_load(info[0:1, 0, ds(i * 4 + c, 1)], min_val=0, max_val=E - 1)
                base = pe.snap(expert * (DT * 2 * INTER))
                pe.wait_ge(xbT_ready, 4 * i + c + 1)
                if c >= 2:
                    pe.wait_ge(ab_ready, 4 * i + c - 1)
                for half, (dst, done) in enumerate(((gate_p, gate_full), (up_p, up_full))):
                    for k in range(DT):
                        mm = nc.tensor.matmul(dst[c % 2][:, :], xbT[:, c % 2, k, :],
                                              w1_flat[:, ds(base + (k * 2 + half) * INTER, INTER)],
                                              start=(k == 0), stop=(k == DT - 1))
                    mm.then_inc(done, 1)

            def turn_act(i, c):
                pe.wait_ge(ab_ready, 4 * i + c + 1)
                if c >= 1:
                    pe.wait_ge(aT_ready, 4 * i + c)
                for k in range(INTER // P):
                    mm = nc.tensor.transpose(at_p[:, k * P:(k + 1) * P], ab[:, c % 2, k * P:(k + 1) * P], ident)
                mm.then_inc(at_full, 1)

            def down(i, c):
                expert = pe.value_load(info[0:1, 0, ds(i * 4 + c, 1)], min_val=0, max_val=E - 1)
                base = pe.snap(expert * (INTER // P * D))
                pe.wait_ge(aT_ready, 4 * i + c + 1)
                if c >= 2:
                    pe.wait_ge(ob_ready, 4 * i + c - 1)
                for k in range(INTER // P):
                    mm = nc.tensor.matmul(out_p[c % 2][:, 0:D], aT[:, c % 2, k * P:(k + 1) * P],
                                          w2_flat[:, ds(base + k * D, D)], start=(k == 0), stop=(k == INTER // P - 1))
                mm.then_inc(out_full, 1)

            pe.wait_ge(info_ready, 1)
            turn_rows(0, 0)
            turn_rows(0, 1)
            pe.wait_ge(w_in, 32)
            up(0, 0)

            def step(i, c):
                turn_act(i, c)
                if c + 2 < NBLK:
                    turn_rows(i, c + 2)
                if c + 1 < NBLK:
                    up(i, c + 1)
                down(i, c)

            blocks(pe, step)

        @block.scalar
        def _(se):
            act_ = nc.scalar.activation

            def prep(m, name):
                if name == "dp":
                    w = filled(se, "prep", m, name)
                    act_(dps[:, :], w[0:R, :], ACT.Copy).then_inc(drained[BANK[name]], 1)
                elif name in ("z0", "z1"):
                    dt = int(name[1])
                    if not (isinstance(m, int) and m == 0):
                        se.wait_ge(lo_ready, DT * m)
                    w = filled(se, "prep", m, name)
                    bias = col("bdt")[:, dt:dt + 1]
                    act_(lnt[:, dt, :], w[:, :], ACT.Abs, bias=bias)
                    act_(rel[:, dt, :], w[:, :], ACT.Relu, bias=bias).then_inc(drained[BANK[name]], 1)
                elif name == "log":
                    drain_of(se, "prep", m, "z1")
                    act_(lnt[:, :, :], lnt[:, :, :], ACT.Exp, scale=-1.0).then_inc(z_exp, 1)
                    se.wait_ge(z_exp, m + 1)
                    act_(lnt[:, :, :], lnt[:, :, :], ACT.Ln, bias=1.0).then_inc(z_log, 1)
                elif name in ("B", "C"):
                    w = filled(se, "prep", m, name)
                    if not (isinstance(m, int) and m < 2):
                        se.wait_ge(hc_ready, NG * (m - 1))
                    o = parity(se, m) * 2 * L + "BC".index(name) * L
                    act_(bc_flat[:, ds(o, L)], w[:, :], ACT.Copy).then_inc(drained[BANK[name]], 1)
                else:
                    i = int(name[2])
                    se.wait_ge((delta_ready, dx_ready)[i], m + 1)
                    if not (isinstance(m, int) and m == 0):
                        se.wait_ge(moved, 128 * m)
                    act_(hi[i][:, :, :], (rel, lnt)[i][:, :, :], ACT.Copy).then_inc(hi_ready, 1)

            def post(m, name):
                if name in ("turn0", "turn1"):
                    i = int(name[4])
                    se.wait_ge(rstd_ready, 2 * m + i + 1)
                    if i == 0:
                        se.wait_ge(xn_out, 16 * (m + 1))
                        se.wait_ge(sums_out, 16 * (m + 1))
                    w = filled(se, "post", m, name)
                    for t in range(2):
                        a = act_(xn4[:, 2 * i + t, :], w[:, t * D:(t + 1) * D], ACT.Identity,
                                 bias=nbias[:, 2 * i + t:2 * i + t + 1], scale=rstd[:, 2 * i + t:2 * i + t + 1])
                    a.then_inc(drained[BANK[name]], 1)
                elif name in ("back0", "back1"):
                    dt = int(name[4])
                    w = filled(se, "post", m, name)
                    act_(xhi[:, dt, :], w[:, :], ACT.Copy).then_inc(xhi_ready, 1)
                elif name == "ex":
                    se.wait_ge(picked, m + 1)
                    act_(ex[:, :], gap[:, :], ACT.Exp).then_inc(ex_ready, 1)
                else:
                    i = int(name[1:])
                    w = filled(se, "post", m, name)
                    act_(th[:, i % 2, :], w[:, :], ACT.Tanh, scale=0.5).then_inc(th_ready, 1)

            def batch(b, with_prep, with_post):
                for n in range(NG):
                    se.wait_ge(decay_in, NG * b + n + 1)
                    act_(da[n % 2][:, :], da[n % 2][:, :], ACT.Exp,
                         scale=aneg[:, n:n + 1]).then_inc(decay_ready, 1)
                    if with_prep:
                        for name in PREP_ACT.get(n, ()):
                            prep(b + 1, name)
                    if with_post:
                        for name in POST_ACT.get(n, ()):
                            post(b - 1, name)

            se.wait_ge(packed, 16)
            act_(aneg[:, :], col("alog"), ACT.Exp).then_inc(const_ready, 1)
            act_(rhi[:, :, :].rearrange("p k e -> p (k e)"), col("rw"), ACT.Copy).then_inc(const_ready, 1)
            act_(lower[:, :, :].rearrange("p k e -> p (k e)"), col("lower"), ACT.Copy).then_inc(const_ready, 1)
            for name in ("dp", "z0", "z1", "log", "B", "C"):
                prep(0, name)
            se.wait_ge(sel_in, 16)
            act_(sel[:, :, :], sel_raw[:, :, :], ACT.Copy).then_inc(const_ready, 1)
            for name in ("hi0", "hi1"):
                prep(0, name)
            se.wait_ge(shared_in, 16)
            for side in range(2):
                act_(wg_hi[:, side, :, :], wg_raw[:, side, :, :], ACT.Copy).then_inc(const_ready, 1)
            se.wait_ge(dconst, 1)
            batch(0, True, False)
            with se.Fori(1, NB - 1) as b:
                batch(b, True, True)
            batch(NB - 1, False, True)
            for n in range(NG):
                for name in POST_ACT.get(n, ()):
                    post(NB - 1, name)

            def rows(i, c):
                se.wait_ge(xt_full, 4 * i + c + 1)
                if c >= 2:
                    se.wait_ge(up_full, 4 * i + c - 1)
                act_(xbT[:, c % 2, :, :].rearrange("p k t -> p (k t)"), xt_p[:, 0:D], ACT.Copy).then_inc(xbT_ready, 1)

            def silu(i, c):
                se.wait_ge(gate_full, 4 * i + c + 1)
                if c >= 2:
                    se.wait_ge(ab_ready, 4 * i + c - 1)
                act_(sg[:, c % 2, :], gate_p[c % 2][:, :], ACT.Silu).then_inc(sg_ready, 1)

            def scale(i, c):
                se.wait_ge(out_full, 4 * i + c + 1)
                if c >= 2:
                    se.wait_ge(added, 16 * (4 * i + c - 1))
                act_(ob[:, c % 2, :], out_p[c % 2][:, 0:D], ACT.Copy,
                     scale=lst[:, c % 4, 1:2].bitcast(F32)).then_inc(ob_ready, 1)

            rows(0, 0)
            rows(0, 1)
            silu(0, 0)

            def step(i, c):
                if c + 2 < NBLK:
                    rows(i, c + 2)
                if c + 1 < NBLK:
                    silu(i, c + 1)
                scale(i, c)

            blocks(se, step)
            for b in range(NB):
                se.wait_ge(fin_rstd, b + 1)
                for t in range(TT):
                    a = act_(fin_o[:, b % 2, t, :], fin[:, b % 2, t, :], ACT.Identity,
                             bias=nbias[:, t:t + 1], scale=rstd[:, t:t + 1])
                a.then_inc(fin_ready, 1)

        @block.vector
        def _(ve_):
            tt = nc.vector.tensor_tensor
            chain = {"k": 0}

            def prep(m, name):
                if name == "delta":
                    ve_.wait_ge(z_log, m + 1)
                    tt(out=rel[:, :, :], in0=rel[:, :, :], in1=lnt[:, :, :], op=ALU.add).then_inc(delta_ready, 1)
                elif name == "dx":
                    t0 = start(ve_, m)
                    ve_.wait_ge(delta_ready, m + 1)
                    if isinstance(m, int):
                        ve_.wait_ge(x_in, 16 * (m + 1))
                    tt(out=lnt[:, :, :], in0=rel[:, :, :], in1=xT[:, :, ds(t0, L)], op=ALU.mult).then_inc(dx_ready, 1)
                else:
                    i = int(name[2])
                    ve_.wait_ge(hi_ready, DT * m + i + 1)
                    if i:
                        ve_.wait_ge(dx_ready, m + 1)
                    if not (isinstance(m, int) and m == 0):
                        ve_.wait_ge(moved, 128 * m)
                    tt(out=lo[i][:, :, :], in0=(rel, lnt)[i][:, :, :], in1=hi[i][:, :, :].bitcast(F32),
                       op=ALU.subtract).then_inc(lo_ready, 1)

            def drive(b, n, bo):
                ve_.wait_ge(drive_in, NG * b + n + 1)
                if n == 0:
                    drain_of(ve_, "prepared", b, "B")
                if not (isinstance(b, int) and NG * b + n < 2):
                    ve_.wait_ge(scanned, NG * b + n - 1)
                tt(out=bx[:, n % 2, :], in0=dxp[n % 2][:, :], in1=bc_flat[:, ds(bo, L)],
                   op=ALU.mult).then_inc(bx_ready, 1)

            def scan(b, n):
                ve_.wait_ge(decay_ready, NG * b + n + 1)
                ve_.wait_ge(bx_ready, NG * b + n + 1)
                if not (isinstance(b, int) and NG * b + n < 4):
                    ve_.wait_ge(hc_ready, NG * b + n - 3)
                nc.vector.tensor_tensor_scan(out=h[:, n % 4, :], data0=da[n % 2][:, :], data1=bx[:, n % 2, :],
                                             initial=0.0, op0=ALU.mult, op1=ALU.add).then_inc(scanned, 1)

            def take_y(b, dt):
                t0 = start(ve_, b)
                ve_.wait_ge(y_quads, NQ * b + 4 * dt + 4)
                nc.vector.scalar_tensor_tensor(out=rT[:, dt, :], in0=xT[:, dt, ds(t0, L)], scalar=dp1[:, dt:dt + 1],
                                               in1=yp[:, :], op0=ALU.mult, op1=ALU.add).then_inc(y_taken, 1)

            def post(m, name):
                def link(instr):
                    chain["k"] += 1
                    instr.then_inc(rt_step, 1)
                    ve_.wait_ge(rt_step, RT_STEPS * m + chain["k"])

                def per_token(ap):
                    return ap.unsqueeze(2).to_broadcast([P, TT, E])

                def per_expert(ap):
                    return ap.unsqueeze(1).to_broadcast([P, TT, E])

                if name in ("turn0", "turn1"):
                    i = int(name[4])
                    w = filled(ve_, "post", m, name)
                    for t in range(2):
                        s = nc.vector.bn_stats(bn[:, 2 * i + t, :], w[:, t * D:(t + 1) * D])
                    s.then_inc(bn_step, 1)
                    ve_.wait_ge(bn_step, 2 * m + i + 1)
                    alone(ve_)
                    for t in range(2):
                        s = nc.vector.bn_aggr(mv[:, 2 * i + t, :], bn[:, 2 * i + t, :])
                    s.then_inc(stats, 1)
                elif name in ("back0", "back1"):
                    dt = int(name[4])
                    ve_.wait_ge(xhi_ready, DT * m + dt + 1)
                    w = filled(ve_, "post", m, name)
                    tt(out=xlo[:, dt, :], in0=w[:, :], in1=xhi[:, dt, :].bitcast(F32),
                       op=ALU.subtract).then_inc(drained[BANK[name]], 1)
                elif name == "logits":
                    chain["k"] = 0
                    w = filled(ve_, "post", m, name)
                    nc.vector.tensor_copy(lg[:, :, :].rearrange("p t e -> p (t e)"),
                                          w[:, 0:TT * E]).then_inc(drained[BANK[name]], 1)
                    drain_of(ve_, "post", m, name)
                    for k in range(2):
                        src = (lg, lg2)[k]
                        link(nc.vector.tensor_reduce(out=mx[:, k, :], in_=src[:, :, :], axis=AX, op=ALU.max))
                        link(tt(out=eq[:, k], in0=src[:, :, :], in1=per_token(mx[:, k, :]), op=ALU.is_equal))
                        link(tt(out=key[:, k], in0=eq[:, k], in1=per_expert(rev), op=ALU.mult))
                        link(nc.vector.tensor_reduce(out=kk[:, k, :], in_=key[:, k], axis=AX, op=ALU.max))
                        link(tt(out=oh[:, k], in0=per_expert(rev), in1=per_token(kk[:, k, :]), op=ALU.is_equal))
                        if k == 0:
                            link(nc.vector.scalar_tensor_tensor(
                                out=lg2[:, :, :], in0=oh[:, 0], scalar=-3e38, in1=lg[:, :, :],
                                op0=ALU.mult, op1=ALU.add))
                    link(tt(out=gap[:, :], in0=mx[:, 1, :], in1=mx[:, 0, :], op=ALU.subtract))
                    tt(out=oh_b[:, :, :], in0=oh[:, 0], in1=oh[:, 1], op=ALU.add).then_inc(picked, 1)
                elif name == "ex":
                    ve_.wait_ge(ex_ready, m + 1)
                    link(nc.vector.tensor_scalar_add(den[:, :], ex[:, :], 1.0))
                    link(nc.vector.reciprocal(sc[:, 0, :], den[:, :]))
                    link(tt(out=sc[:, 1, :], in0=ex[:, :], in1=sc[:, 0, :], op=ALU.mult))
                elif name == "ranks":
                    w = filled(ve_, "post", m, name)
                    tot = w[:, TT * E:2 * TT * E].rearrange("p (t e) -> p t e", e=E)
                    for t in range(TT):
                        link(tt(out=offs[:, t + 1, :], in0=offs[:, t, :], in1=tot[:, t, :], op=ALU.add))
                    tt(out=rk[:, :, :], in0=w[:, 0:TT * E].rearrange("p (t e) -> p t e", e=E),
                       in1=offs[:, 0:TT, :], op=ALU.add).then_inc(drained[BANK[name]], 1)
                    drain_of(ve_, "post", m, name)
                    link(nc.vector.tensor_copy(offs[:, 0, :], offs[:, TT, :]))
                    link(tt(out=rk2[:, :, :], in0=rk[:, :, :], in1=per_expert(region), op=ALU.add))
                    t0 = m * TT if isinstance(m, int) else ve_.snap(m * TT)
                    for k in range(2):
                        link(tt(out=pr[:, k], in0=oh[:, k], in1=rk2[:, :, :], op=ALU.mult))
                        link(nc.vector.tensor_reduce(out=posf[:, k, :], in_=pr[:, k], axis=AX, op=ALU.add))
                        link(nc.vector.tensor_copy(ent[:, k, :, 1:2].bitcast(F32), sc[:, k, :].unsqueeze(2)))
                        alone(ve_)
                        link(nc.vector.tensor_copy(ent[:, k, :, 0:1], tok[:, ds(t0, TT)].unsqueeze(2)))
                    assert chain["k"] == RT_STEPS, chain
                    nc.vector.tensor_copy(pos[:, :, :], posf[:, :, :]).then_inc(ent_ready, 1)
                elif name[0] == "g":
                    i = int(name[1:])
                    ve_.wait_ge(th_ready, NI * m + i + 1)
                    w = filled(ve_, "post", m, name)
                    nc.vector.scalar_tensor_tensor(out=act[:, i, :], in0=th[:, i % 2, :], scalar=1.0, in1=w[:, :],
                                                   op0=ALU.add, op1=ALU.mult).then_inc(drained[BANK[name]], 1)
                elif name[0] == "u":
                    i = int(name[1:])
                    drain_of(ve_, "post", m, f"g{i}")
                    w = filled(ve_, "post", m, name)
                    nc.vector.scalar_tensor_tensor(out=act[:, i, :], in0=act[:, i, :], scalar=0.5, in1=w[:, :],
                                                   op0=ALU.mult, op1=ALU.mult).then_inc(drained[BANK[name]], 1)
                else:
                    i = int(name[4])
                    ve_.wait_ge(xn_out, 16 * (m + 2))
                    w = filled(ve_, "post", m, name)
                    o = xn4[:, 2 * i:2 * i + 2, :].rearrange("p t d -> p (t d)")
                    tt(out=o, in0=w[:, :], in1=o, op=ALU.add).then_inc(drained[BANK[name]], 1)

            def batch(b, with_prep, with_post):
                bo = parity(ve_, b) * 2 * L
                if not isinstance(bo, int):
                    bo = ve_.snap(bo)
                drive(b, 0, bo)
                for n in range(NG):
                    if n + 1 < NG:
                        drive(b, n + 1, bo)
                    scan(b, n)
                    if with_post and n == Y1_AT:
                        take_y(b - 1, 1)
                    if n == Y0_AT:
                        take_y(b, 0)
                    if with_prep:
                        for name in PREP_DVE.get(n, ()):
                            prep(b + 1, name)
                    if with_post:
                        for name in POST_DVE.get(n, ()):
                            post(b - 1, name)

            nc.vector.memset(mhalf[:, :], -0.5).then_inc(dconst, 1)
            nc.vector.memset(offs[:, 0, :], 0.0).then_inc(dconst, 1)
            nc.vector.memset(xn4[:, 0, :], 0.0).then_inc(dconst, 1)
            for name in ("delta", "dx", "lo0", "lo1"):
                prep(0, name)
            ve_.wait_ge(const_ready, SETUP_ACT)
            nc.vector.tensor_scalar_mul(aneg[:, :], aneg[:, :], -1.0).then_inc(dconst, 1)
            nc.vector.tensor_scalar_add(dp1[:, :], col("dpar"), 1.0).then_inc(dconst, 1)
            tt(out=rlo[:, :, :].rearrange("p k e -> p (k e)"), in0=col("rw"),
               in1=rhi[:, :, :].rearrange("p k e -> p (k e)").bitcast(F32), op=ALU.subtract).then_inc(dconst, 1)
            for side in range(2):
                tt(out=wg_lo[:, side, :, :], in0=wg_raw[:, side, :, :], in1=wg_hi[:, side, :, :].bitcast(F32),
                   op=ALU.subtract).then_inc(dconst, 1)
            ve_.wait_ge(dconst, SETUP_DVE)
            batch(0, True, False)
            with ve_.Fori(1, NB - 1) as b:
                batch(b, True, True)
            batch(NB - 1, False, True)
            take_y(NB - 1, 1)
            for n in range(NG):
                for name in POST_DVE.get(n, ()):
                    post(NB - 1, name)

            blk = {"k": 0}

            def link(instr):
                blk["k"] += 1
                instr.then_inc(info_step, 1)
                ve_.wait_ge(info_step, blk["k"])

            def by_expert(ap):
                return ap.unsqueeze(1).to_broadcast([1, NBLK, E])

            def by_block(ap):
                return ap.unsqueeze(2).to_broadcast([1, NBLK, E])

            number, expert = col("block", 1), col("expert", 1)
            link(nc.vector.tensor_scalar_add(cnti[:, 0, :], offs[0:1, 0, :], float(P - 1)))
            link(nc.vector.tensor_single_scalar(cnti[:, 1, :], cnti[:, 0, :], 7, op=ALU.arith_shift_right))
            link(nc.vector.tensor_copy(cnt[:, 0, :], cnti[:, 1, :]))
            link(nc.vector.memset(cnt[:, 1, :], 1.0))
            link(nc.vector.tensor_tensor_scan(out=cnt[:, 2, :], data0=cnt[:, 1, :], data1=cnt[:, 0, :],
                                              initial=0.0, op0=ALU.mult, op1=ALU.add))
            link(tt(out=cnt[:, 3, :], in0=cnt[:, 2, :], in1=cnt[:, 0, :], op=ALU.subtract))
            link(tt(out=btw[:, :, :], in0=by_block(number), in1=by_expert(cnt[:, 2, :]), op=ALU.is_ge))
            link(nc.vector.tensor_reduce(out=btc[:, 0, :], in_=btw[:, :, :], axis=AX, op=ALU.add))
            link(nc.vector.tensor_scalar(out=btc[:, 1, :], in0=btc[:, 0, :], scalar1=float(E), scalar2=None,
                                         op0=ALU.is_lt))
            link(nc.vector.tensor_scalar(out=btc[:, 2, :], in0=btc[:, 0, :], scalar1=float(E - 1), scalar2=None,
                                         op0=ALU.min))
            link(tt(out=btw[:, :, :], in0=by_expert(expert), in1=by_block(btc[:, 2, :]), op=ALU.is_equal))
            link(tt(out=btw[:, :, :], in0=btw[:, :, :], in1=by_expert(cnt[:, 3, :]), op=ALU.mult))
            link(nc.vector.tensor_reduce(out=btc[:, 3, :], in_=btw[:, :, :], axis=AX, op=ALU.add))
            link(tt(out=btc[:, 4, :], in0=number, in1=btc[:, 3, :], op=ALU.subtract))
            link(nc.vector.tensor_scalar(out=btc[:, 5, :], in0=btc[:, 4, :], scalar1=float(P),
                                         scalar2=-float(E * REGION), op0=ALU.mult, op1=ALU.add))
            link(nc.vector.scalar_tensor_tensor(out=btc[:, 6, :], in0=btc[:, 2, :], scalar=float(REGION),
                                                in1=btc[:, 5, :], op0=ALU.mult, op1=ALU.add))
            link(tt(out=btc[:, 7, :], in0=btc[:, 6, :], in1=btc[:, 1, :], op=ALU.mult))
            link(nc.vector.tensor_copy(info[:, 0, :], btc[:, 2, :]))
            nc.vector.tensor_scalar_add(info[:, 1, :], btc[:, 7, :], float(E * REGION)).then_inc(info_ready, 1)

            def gated(i, c):
                ve_.wait_ge(sg_ready, 4 * i + c + 1)
                ve_.wait_ge(up_full, 4 * i + c + 1)
                if c >= 2:
                    ve_.wait_ge(at_full, 4 * i + c - 1)
                tt(out=ab[:, c % 2, :], in0=up_p[c % 2][:, :], in1=sg[:, c % 2, :], op=ALU.mult).then_inc(ab_ready, 1)

            def turned(i, c):
                ve_.wait_ge(at_full, 4 * i + c + 1)
                if c >= 2:
                    ve_.wait_ge(out_full, 4 * i + c - 1)
                nc.vector.tensor_copy(aT[:, c % 2, :], at_p[:, :]).then_inc(aT_ready, 1)

            gated(0, 0)

            def step(i, c):
                turned(i, c)
                if c + 1 < NBLK:
                    gated(i, c + 1)

            blocks(ve_, step)
            for b in range(NB):
                ve_.wait_ge(fin_in[b % 2], 16 * (b // 2 + 1))
                if b:
                    ve_.wait_ge(stats, 2 * NB + b)
                for t in range(TT):
                    s = nc.vector.bn_stats(bn[:, t, :], fin[:, b % 2, t, :])
                s.then_inc(bn_step, 1)
                ve_.wait_ge(bn_step, 2 * NB + b + 1)
                if b:
                    ve_.wait_ge(fin_rstd, b)
                for t in range(TT):
                    s = nc.vector.bn_aggr(mv[:, t, :], bn[:, t, :])
                s.then_inc(stats, 1)

        @block.gpsimd
        def _(po):
            def rstd_of(lo_, hi_, done, k):
                r = slice(lo_, hi_)
                var, mean = mv[:, r, 1:2].squeeze(2), mv[:, r, 0:1].squeeze(2)
                alone(po)
                po.tensor_scalar(out=ve[:, r], in0=var, scalar1=EPS, scalar2=None, op0=ALU.add).then_inc(rs_step, 1)
                po.wait_ge(rs_step, 2 * k + 1)
                po.tensor_tensor(out=rstd[:, r], in0=ve[:, r], in1=mhalf[:, r], op=ALU.pow)
                po.tensor_scalar(out=nbias[:, r], in0=mean, scalar1=-1.0, scalar2=None, op0=ALU.mult).then_inc(rs_step, 1)
                po.wait_ge(rs_step, 2 * k + 2)
                alone(po)
                po.tensor_tensor(out=nbias[:, r], in0=nbias[:, r], in1=rstd[:, r], op=ALU.mult).then_inc(done, 1)

            def post(m, name):
                if name in ("turn0", "turn1"):
                    i = int(name[4])
                    po.wait_ge(stats, 2 * m + i + 1)
                    rstd_of(2 * i, 2 * i + 2, rstd_ready, 2 * m + i)
                elif name == "landed":
                    po.wait_ge(scattered, 128 * (m + 1))
                    alone(po)
                else:
                    po.wait_ge(ent_ready, m + 1)
                    alone(po)
                    for k in range(2):
                        for t in range(TT):
                            po.indirect_dma_start(out=list_d, in_=ent[:, k, t, :], in_offset=None,
                                                  out_offset=bass.IndirectOffsetOnAxis(ap=pos[:, k, t:t + 1], axis=0)
                                                  ).then_inc(scattered, 16)

            def batch(b, with_post):
                co = parity(po, b) * 2 * L + L
                if not isinstance(co, int):
                    co = po.snap(co)
                for n in range(NG):
                    po.wait_ge(scanned, NG * b + n + 1)
                    if n == 0:
                        drain_of(po, "prepared", b, "C")
                    if not (isinstance(b, int) and NG * b + n < 8):
                        po.wait_ge(y_quads, NQ * b + (n - 8) // 4 + 1)
                    alone(po)
                    po.tensor_tensor(out=hc[:, n % 8, :], in0=h[:, n % 4, :], in1=bc_flat[:, ds(co, L)],
                                     op=ALU.mult).then_inc(hc_ready, 1)
                    if with_post:
                        for name in POST_POOL.get(n, ()):
                            post(b - 1, name)

            po.wait_ge(dconst, 3)
            po.wait_ge(padded, 16)
            batch(0, False)
            with po.Fori(1, NB - 1) as b:
                batch(b, True)
            batch(NB - 1, True)
            for n in range(NG):
                for name in POST_POOL.get(n, ()):
                    post(NB - 1, name)

            def gather(i, c):
                po.wait_ge(list_in[c % 4], 16 * i + 16 * (c // 4 + 1))
                if c >= 4:
                    po.wait_ge(xt_full, 4 * i + c - 3)
                alone(po)
                po.indirect_dma_start(out=xb[:, c % 4, :], out_offset=None, in_=xn_d,
                                      in_offset=bass.IndirectOffsetOnAxis(ap=lst[:, c % 4, 0:1], axis=0)
                                      ).then_inc(rows_in[c % 4], 16)

            def add(i, c):
                po.wait_ge(ob_ready, 4 * i + c + 1)
                if c >= 1:
                    po.wait_ge(added, 16 * (4 * i + c))
                alone(po)
                po.indirect_dma_start(out=acc_d, in_=ob[:, c % 2, :], in_offset=None, compute_op=ALU.add,
                                      out_offset=bass.IndirectOffsetOnAxis(ap=lst[:, c % 4, 0:1], axis=0)
                                      ).then_inc(added, 16)

            po.wait_ge(xn_out, 16 * (NB + 1))
            for c in range(3):
                gather(0, c)
            po.wait_ge(sums_out, 16 * (NB + 1))

            def step(i, c):
                if c + 3 < NBLK:
                    gather(i, c + 3)
                add(i, c)

            blocks(po, step)
            for b in range(NB):
                po.wait_ge(stats, 2 * NB + b + 1)
                if b:
                    po.wait_ge(fin_ready, b)
                rstd_of(0, TT, fin_rstd, 2 * NB + b)

        @block.sync
        def _(sp):
            sp.dma_start(pk[:, :], A["pack"]).then_inc(packed, 16)
            sp.dma_start(xT[:, :, 0:L], A["xT"][:, :, 0:L]).then_inc(x_in, 16)
            sp.dma_start(wdt[:, :], A["wdt"]).then_inc(wdt_in, 16)
            sp.dma_start(sel_raw[:, :, :], A["sel"]).then_inc(sel_in, 16)
            sp.dma_start(wg_raw[:, :, :, :], A["wgu"]).then_inc(shared_in, 16)
            sp.dma_start(tok[:, :], A["tok"]).then_inc(tok_in, 16)
            for b in range(1, NB):
                sp.wait_ge(x_in, 16 * b)
                sp.dma_start(xT[:, :, b * L:(b + 1) * L], A["xT"][:, :, b * L:(b + 1) * L]).then_inc(x_in, 16)
            sp.dma_start(list_d, A["list"]).then_inc(padded, 16)
            sp.wait_ge(dconst, 3)
            sp.dma_start(xn_d[T:T + P, :], xn4[:, 0, :]).then_inc(xn_out, 16)
            sp.dma_start(acc_d[T:T + P, :], xn4[:, 0, :]).then_inc(sums_out, 16)
            sp.dma_start(wd[:, :, :], A["wd"]).then_inc(down_in, 16)

            def moves(m):
                par = parity(sp, m)
                sp.wait_ge(lo_ready, DT * (m + 1))
                alone(sp)
                if not (isinstance(m, int) and m < 2):
                    sp.wait_ge(drive_in, NG * (m - 1))
                    alone(sp)
                for i in range(2):
                    for side, src in ((0, hi[i]), (1, lo[i])):
                        for up_ in range(2):
                            to = slice(64 * (up_ ^ side), 64 * (up_ ^ side) + 64)
                            dst = hl[i][to, ds(par, 1), up_::2, :].rearrange("p a c l -> p (a c) l")
                            sp.dma_start(dst.bitcast(F32), src[64 * up_:64 * up_ + 64, :, :].bitcast(F32)
                                         ).then_inc(moved, 16)

            def rows_of(table, m):
                return table[ds(start(sp, m), L), :].rearrange("(t p) d -> p t d", p=P)

            def store(m, name):
                dst = rows_of((xn_d, acc_d)[name == "down1"], m)
                drain_of(sp, "post", m, name)
                alone(sp)
                sp.dma_start(dst, xn4[:, :, :]).then_inc((xn_out, sums_out)[name == "down1"], 16)

            moves(0)
            moves(1)
            with sp.Fori(1, NB - 1) as b:
                store(b - 1, "turn1")
                moves(b + 1)
                store(b - 1, "down1")
            for m in (NB - 2, NB - 1):
                store(m, "turn1")
                store(m, "down1")
            sp.wait_ge(y_taken, DT * NB)
            sp.dma_start(w1[:, :, :, :], A["w1"]).then_inc(w_in, 16)
            sp.dma_start(w2[:, :, :, :], A["w2"]).then_inc(w_in, 16)
            sp.wait_ge(info_ready, 1)
            sp.wait_ge(scattered, 128 * NB)

            def fetch(i, c):
                row = sp.value_load(info[0:1, 1, ds(i * 4 + c, 1)], min_val=0, max_val=NLIST - P)
                if c >= 4:
                    sp.wait_ge(added, 16 * (4 * i + c - 3))
                    alone(sp)
                sp.dma_start(lst[:, c % 4, :], list_d[ds(row, P), :]).then_inc(list_in[c % 4], 16)

            for c in range(3):
                fetch(0, c)

            def step(i, c):
                if c + 3 < NBLK:
                    fetch(i, c + 3)

            blocks(sp, step)
            sp.wait_ge(added, 16 * NBLK)
            for b in range(NB):
                if b >= 2:
                    sp.wait_ge(fin_ready, b - 1)
                sp.dma_start(fin[:, b % 2, :, :],
                             acc_d[b * L:(b + 1) * L, :].rearrange("(t p) d -> p t d", p=P)).then_inc(fin_in[b % 2], 16)
                if b:
                    sp.wait_ge(fin_ready, b)
                    sp.dma_start(out[(b - 1) * L:b * L, :].rearrange("(t p) d -> p t d", p=P),
                                 fin_o[:, (b - 1) % 2, :, :]).then_inc(fin_out, 16)
            sp.wait_ge(fin_ready, NB)
            sp.dma_start(out[(NB - 1) * L:, :].rearrange("(t p) d -> p t d", p=P),
                         fin_o[:, (NB - 1) % 2, :, :]).then_inc(fin_out, 16)
            sp.wait_ge(fin_out, 16 * NB)


def kernel(**inputs):
    import concourse.bacc as _bacc
    from concourse.bass_utils import run_bass_kernel_spmd as _run

    x = np.asarray(inputs["L0_attn_x"])
    w_x, w_dt = np.asarray(inputs["L0_attn_W_x"]), np.asarray(inputs["L0_attn_W_dt"])

    def tiles(a):
        return np.ascontiguousarray(a.reshape(-1, P, a.shape[-1]).transpose(1, 0, 2))

    def bc_rows(a):
        return tiles(np.repeat(a.T, GC, axis=1)).reshape(P, DT * P)

    a_log = np.asarray(inputs["L0_attn_A_log"]).reshape(DT, 4, 4, GC, NS).transpose(4, 3, 0, 2, 1).reshape(P, NG)
    parts = {
        "wp": tiles(w_x[:R].T).reshape(P, -1),
        "wbc": np.concatenate([bc_rows(w_x[R:R + NS]), bc_rows(w_x[R + NS:])], axis=1),
        "bdt": np.asarray(inputs["L0_attn_b_dt"]).reshape(DT, P).T,
        "dpar": np.asarray(inputs["L0_attn_D"]).reshape(DT, P).T,
        "alog": a_log,
        "rw": tiles(np.asarray(inputs["L0_ffn_router_w"])).reshape(P, -1),
    }
    row = np.arange(P)
    state, chan = row // GC, row % GC
    ysel = np.zeros((P, 4, 32), np.float32)
    for k in range(4):
        ysel[row, k, GC * k + chan] = 1
    sel = np.zeros((P, 8, P), np.float32)
    for j in range(8):
        sel[:, j, :] = (row[:, None] % 64) == (GC * j + chan)[None, :]
    parts["ysel"] = ysel.reshape(P, -1)
    parts["ident"] = np.eye(P, dtype=np.float32)
    parts["lower"] = np.concatenate([np.triu(np.ones((P, P), np.float32), 1), np.ones((P, P), np.float32)], axis=1)
    for name, v in (("rev", E - np.arange(E)), ("region", REGION * np.arange(E)), ("expert", np.arange(E)),
                    ("block", np.arange(NBLK))):
        parts[name] = np.tile(v.astype(np.float32), (P, 1))
    slots = np.zeros((NLIST, 2), np.int32)
    slots[:, 0] = TRASH + np.arange(NLIST) % P
    arrays = {
        "pack": np.ascontiguousarray(np.concatenate([parts[n] for n, _ in PACK], axis=1)),
        "xT": tiles(x.reshape(T, D).T),
        "wdt": np.ascontiguousarray(w_dt.T),
        "sel": sel,
        "wgu": np.ascontiguousarray(np.stack([tiles(np.asarray(inputs["L0_ffn_w_gate"])),
                                              tiles(np.asarray(inputs["L0_ffn_w_up"]))], axis=1)),
        "wd": tiles(np.asarray(inputs["L0_ffn_w_down"])),
        "w1": np.ascontiguousarray(np.asarray(inputs["L0_ffn_w1"]).reshape(E, DT, P, 2 * INTER).transpose(2, 0, 1, 3)),
        "w2": np.ascontiguousarray(np.asarray(inputs["L0_ffn_w2"]).reshape(E, INTER // P, P, D).transpose(2, 0, 1, 3)),
        "tok": np.ascontiguousarray((row[:, None] + P * np.arange(T // P)[None, :]).astype(np.int32)),
        "list": slots,
    }
    nc = _bacc.Bacc("TRN2", target_bir_lowering=False, num_devices=1)
    args = {n: nc.dram_tensor(f"in_{n}", a.shape, mybir.dt.from_np(a.dtype), kind="ExternalInput").ap()
            for n, a in arrays.items()}
    out = nc.dram_tensor("out", (T, D), F32, kind="ExternalOutput").ap()
    program(nc, args, out)
    r = _run(nc, [{f"in_{n}": a for n, a in arrays.items()}], core_ids=[0])
    return r.results[0]["out"].reshape(x.shape)
```

```python
from contextlib import ExitStack

import numpy as np
import concourse.bass as bass
from concourse import mybir

P = 128
NB = 4
L = 512
T = NB * L
D = 256
DT = D // P
NS = 16
GC = P // NS
NG = D // GC
NQ = NG // 4
R = 64
TT = L // P
E = 8
INTER = 512
SI = 1024
NI = SI // P
NBLK = (2 * T) // P + E - 1
REGION = T
NLIST = E * REGION + P
TRASH = T
EPS = 1e-5

F32 = mybir.dt.float32
F32R = mybir.dt.float32r
BF16 = mybir.dt.bfloat16
I32 = mybir.dt.int32
ACT = mybir.ActivationFunctionType
ALU = mybir.AluOpType
AX = mybir.AxisListType.X
ds = bass.ds

PREP = ["dp", "z0", "z1", "B", "C"]
ORDER = (["dp", "z0", "z1", "turn0", "turn1", "B", "C", "back0", "back1", "logits",
          "g0", "u0", "g1", "u1", "g2", "u2", "g3", "u3", "ranks"]
         + [f"{w}{i}" for i in range(4, NI) for w in "gu"] + ["down0", "down1"])
POST = [n for n in ORDER if n not in PREP]
BANK = {n: k % 3 for k, n in enumerate(ORDER)}

PREP_AT = {0: ["dp"], 2: ["z0", "z1"], 5: ["B"], 8: ["C"]}
POST_AT = {4: ["turn0", "turn1"], 9: ["back0", "back1"], 12: ["logits", "g0"], 13: ["u0"], 14: ["g1"], 15: ["u1"],
           16: ["g2"], 17: ["u2"], 18: ["g3"], 19: ["u3", "ranks"], 20: ["g4"], 21: ["u4"], 22: ["g5"], 23: ["u5"],
           24: ["g6"], 25: ["u6"], 26: ["g7"], 27: ["u7"], 28: ["down0"], 30: ["down1"]}
PREP_ACT = {1: ["dp"], 3: ["z0", "z1"], 4: ["log"], 6: ["B"], 9: ["C"], 11: ["hi0"], 12: ["hi1"]}
POST_ACT = {7: ["turn0", "turn1"], 10: ["back0", "back1"], 13: ["g0"], 15: ["g1"], 17: ["g2", "ex"],
            19: ["g3"], 21: ["g4"], 23: ["g5"], 25: ["g6"], 27: ["g7"]}
PREP_DVE = {7: ["delta"], 8: ["dx"], 11: ["lo0"], 12: ["lo1"]}
POST_DVE = {4: ["turn0", "turn1"], 10: ["back0", "back1"], 12: ["logits"], 13: ["g0", "u0"], 14: ["first"],
            15: ["g1", "u1"], 16: ["second"], 17: ["g2", "u2"], 18: ["ex"], 19: ["g3", "u3"], 20: ["ranks"],
            21: ["g4", "u4"], 22: ["rows0"], 23: ["g5", "u5"], 24: ["rows1"],
            25: ["g6", "u6"], 27: ["g7", "u7"], 29: ["down0"], 31: ["down1"]}
POST_POOL = {4: ["turn0", "turn1"], 31: ["landed"],
             **{25 + j: [f"scatter{2 * j}", f"scatter{2 * j + 1}"] for j in range(4)}}
SHARED_ACT = {14: 0, 16: 1, 18: 2, 20: 3}
SHARED_DVE = {15: 0, 17: 1, 19: 2, 21: 3}
LAST_QUAD_AT = 2
Y1_AT, Y0_AT = 2, 20
RT_STEPS = 30
SCAN_ACT, SETUP_ACT, SCAN_DVE, SETUP_DVE = 4, 8, 6, 10


def in_bank(k, names):
    return sum(BANK[n] == k for n in names)


def uses(stage, m, name):
    k = BANK[name]
    before = ORDER[:ORDER.index(name)]
    if stage == "prep":
        with_post = not isinstance(m, int) or m >= 2
        base = m * in_bank(k, PREP) + ((m - 2) * in_bank(k, POST) if with_post else 0)
        beside = PREP if not with_post else ORDER
    else:
        with_prep = not isinstance(m, int) or m < 2
        base = m * in_bank(k, POST) + ((m + 2) * in_bank(k, PREP) if with_prep else NB * in_bank(k, PREP))
        beside = POST if not with_prep else ORDER
    return base + in_bank(k, [n for n in before if n in beside]) + 1


def uses_before(b, k):
    p, q = in_bank(k, PREP), in_bank(k, POST)
    return p if isinstance(b, int) and b == 0 else (b + 1) * p + (b - 1) * q


PACK = [("wp", DT * R), ("wbc", 2 * DT * P), ("bdt", DT), ("dpar", DT), ("alog", NG), ("ysel", 4 * 32),
        ("ident", P), ("lower", 2 * P), ("rw", DT * E), ("rev", E), ("region", E), ("expert", E), ("block", NBLK)]
COL = {}
for _name, _n in PACK:
    COL[_name] = (sum(n for _, n in COL.values()) if COL else 0, _n)
NPACK = sum(n for _, n in PACK)


def program(nc, A, out):
    xn_d = nc.dram_tensor("xn_rows", [T + P, D], F32).ap()
    acc_d = nc.dram_tensor("acc_rows", [T + P, D], F32).ap()
    list_d = nc.dram_tensor("slot_list", [NLIST, 2], I32).ap()

    with ExitStack() as ctx:
        top = [(nc.sbuf_base + 63) // 64 * 64]

        def at(name, shape, dt=F32, offset=None):
            size = int(np.prod(shape[1:])) * (2 if dt == BF16 else 4)
            if offset is None:
                offset = top[0]
                top[0] += (size + 31) // 32 * 32
            return nc.alloc_sbuf_tensor_at(name, shape, dt, offset=offset)

        def sem(name):
            return ctx.enter_context(nc.semaphore(name))

        pk = at("pack", [P, NPACK])

        def col(name, rows=P):
            o, n = COL[name]
            return pk[0:rows, o:o + n]

        ident = col("ident")
        rev, region = col("rev"), col("region")
        lower = at("lower", [P, 2, P], BF16)
        tok = at("tok", [P, T // P], I32)
        bn = at("bn", [P, TT, 6])
        mv = at("mv", [P, TT, 2])
        ve = at("ve", [P, TT])
        mhalf = at("mhalf", [P, TT])
        rstd = at("rstd", [P, TT])
        nbias = at("nbias", [P, TT])
        offs = at("offs", [P, TT + 1, E])
        lst_rows = at("lst_rows", [P, 4, 2], I32)
        lst = at("lst", [P, 4, 2], I32)
        lg = at("lg", [P, TT, E])
        lg2 = at("lg2", [P, TT, E])
        eq = at("eq", [P, 2, TT, E])
        key = at("key", [P, 2, TT, E])
        oh = at("oh", [P, 2, TT, E])
        oh_b = at("oh_b", [P, TT, E], BF16)
        rk = at("rk", [P, TT, E])
        rk2 = at("rk2", [P, TT, E])
        pr = at("pr", [P, 2, TT, E])
        mx = at("mx", [P, 2, TT])
        kk = at("kk", [P, 2, TT])
        gap = at("gap", [P, TT])
        ex = at("ex", [P, TT])
        den = at("den", [P, TT])
        sc = at("sc", [P, 2, TT])
        posf = at("posf", [P, 2, TT])
        pos = at("pos", [P, 2, TT], I32)
        ent = at("ent", [P, 2, TT, 2], I32)
        rw = at("rw", [P, DT, 2, E], F32R)
        cnt = at("cnt", [1, 5, E])
        cnti = at("cnti", [1, 2, E], I32)
        btw = at("btw", [1, NBLK, E])
        btc = at("btc", [1, 8, NBLK])
        info = at("info", [1, 2, NBLK], I32)
        rT = at("rT", [P, DT, L])
        xn4 = at("xn4", [P, TT, D])
        xhi = at("xhi", [P, DT, L], F32R)
        xlo = at("xlo", [P, DT, L], F32R)
        th_offset = top[0]
        th = at("th", [P, 2, L])
        act_offset = top[0]
        act = at("act", [P, NI, L])
        wg_hi = at("wg_hi", [P, 2, DT, SI], F32R)
        wg_lo = at("wg_lo", [P, 2, DT, SI], F32R)
        wd = at("wd", [P, NI, D])
        sel_raw = at("sel_raw", [P, 8, P], F32, th_offset)
        wg_raw = at("wg_raw", [P, 2, DT, SI], F32, act_offset)
        epoch = top[0]
        xT = at("xT", [P, DT, T])
        hl = [at("hl_delta", [P, 2, 4, L], F32R), at("hl_dx", [P, 2, 4, L], F32R)]
        bc = at("bc", [P, 2, 2, L])
        rel = at("rel", [P, DT, L])
        lnt = at("lnt", [P, DT, L])
        hi = [at("hi_delta", [P, DT, L], F32R), at("hi_dx", [P, DT, L], F32R)]
        lo = [at("lo_delta", [P, DT, L], F32R), at("lo_dx", [P, DT, L], F32R)]
        dps = at("dps", [R, L])
        bx = at("bx", [P, 2, L])
        h = at("h", [P, 4, L])
        hc = at("hc", [P, 8, L])
        sel = at("sel", [P, 8, P], F32R)
        wdt = at("wdt", [R, D])
        aneg = at("aneg", [P, NG])
        dp1 = at("dp1", [P, DT])
        end_scan = top[0]
        assert end_scan <= nc.sbuf_usable_end, (end_scan, nc.sbuf_usable_end)
        top[0] = epoch
        w1 = at("w1", [P, E, DT, 2 * INTER])
        w2 = at("w2", [P, E, INTER // P, D])
        xb = at("xb", [P, 4, D])
        xbT = at("xbT", [P, 2, DT, P])
        sg = at("sg", [P, 2, INTER])
        ab = at("ab", [P, 2, INTER])
        aT = at("aT", [P, 2, INTER])
        ob = at("ob", [P, 2, D])
        after = top[0]
        top[0] = epoch
        fin = at("fin", [P, NB, TT, D])
        fin_o = at("fin_o", [P, NB, TT, D])
        fin_bn = at("fin_bn", [P, NB * TT, 6])
        fin_mv = at("fin_mv", [P, NB * TT, 2])
        fin_ve = at("fin_ve", [P, NB * TT])
        fin_rs = at("fin_rs", [P, NB * TT])
        fin_nb = at("fin_nb", [P, NB * TT])
        fin_half = at("fin_half", [P, NB * TT])
        assert top[0] <= epoch + E * DT * 2 * INTER * 4
        top[0] = after
        assert top[0] <= nc.sbuf_usable_end
        bank = [ctx.enter_context(nc.psum_tensor(f"bank{k}", [P, L], F32)) for k in range(8)]
        da, dxp, yp, work = bank[0:2], bank[2:4], bank[4], bank[5:8]
        gate_p, up_p = [bank[0], bank[2]], [bank[1], bank[3]]
        xt_p, at_p, out_p = bank[4], bank[5], bank[6:8]

        packed = sem("packed")
        x_in = sem("x_in")
        sel_in = sem("sel_in")
        wdt_in = sem("wdt_in")
        shared_in = sem("shared_in")
        down_in = sem("down_in")
        tok_in = sem("tok_in")
        const_ready = sem("const_ready")
        dconst = sem("dconst")
        full = [sem(f"work_full{k}") for k in range(3)]
        drained = [sem(f"work_drained{k}") for k in range(3)]
        z_exp = sem("z_exp")
        z_log = sem("z_log")
        delta_ready = sem("delta_ready")
        dx_ready = sem("dx_ready")
        hi_ready = sem("hi_ready")
        lo_ready = sem("lo_ready")
        moved = sem("moved")
        decay_in = sem("decay_in")
        drive_in = sem("drive_in")
        decay_ready = sem("decay_ready")
        bx_ready = sem("bx_ready")
        scanned = sem("scanned")
        hc_ready = sem("hc_ready")
        y_quads = sem("y_quads")
        y_taken = sem("y_taken")
        stats = sem("stats")
        bn_step = sem("bn_step")
        rs_step = sem("rs_step")
        rstd_ready = sem("rstd_ready")
        xn_out = sem("xn_out")
        xhi_ready = sem("xhi_ready")
        picked = sem("picked")
        ex_ready = sem("ex_ready")
        rt_step = sem("rt_step")
        ent_ready = sem("ent_ready")
        scattered = sem("scattered")
        th_ready = sem("th_ready")
        sums_out = sem("sums_out")
        info_ready = sem("info_ready")
        w1_in = sem("w1_in")
        w2_in = sem("w2_in")
        row_list_in = [sem(f"row_list_in{k}") for k in range(4)]
        list_in = [sem(f"list_in{k}") for k in range(4)]
        rows_in = [sem(f"rows_in{k}") for k in range(4)]
        xt_full = sem("xt_full")
        xbT_ready = sem("xbT_ready")
        gate_full = sem("gate_full")
        up_full = sem("up_full")
        sg_ready = sem("sg_ready")
        ab_ready = sem("ab_ready")
        at_full = sem("at_full")
        aT_ready = sem("aT_ready")
        out_full = sem("out_full")
        ob_ready = sem("ob_ready")
        added = sem("added")
        fin_in = [sem(f"fin_in{k}") for k in range(NB)]
        fin_rstd = sem("fin_rstd")
        padded = sem("padded")
        passed = sem("passed")
        info_step = sem("info_step")
        fin_ready = sem("fin_ready")
        fin_out = sem("fin_out")
        block = ctx.enter_context(nc.Block())

        hl_flat = [t[:, :, :, :].rearrange("p a c l -> p (a c l)") for t in hl]
        bc_flat = bc[:, :, :, :].rearrange("p a s l -> p (a s l)")

        def geometry(n):
            dt, s = divmod(n, NG // DT)
            q, k = s % 4, s // 4
            return dt, q, k, 2 * dt + q // 2, (q % 2) * 4 + k

        def parity(eng, m):
            return m % 2 if isinstance(m, int) else eng.snap(m % 2)

        def filled(eng, stage, m, name):
            eng.wait_ge(full[BANK[name]], uses(stage, m, name))
            return work[BANK[name]]

        def drain_of(eng, stage, m, name):
            eng.wait_ge(drained[BANK[name]], uses(stage, m, name))

        def wait_prepared(eng, b, name):
            eng.wait_ge(drained[BANK[name]], uses_before(b, BANK[name]))

        def alone(eng):
            eng.sem_inc(passed, 1)

        def blocks(eng, step):
            rounds = (NBLK - 5) // 4 - 1
            for c in range(4):
                step(0, c)
            with eng.Fori(0, rounds) as i:
                for c in range(4, 8):
                    step(i, c)
            for c in range(4 * rounds + 4, NBLK):
                step(0, c)

        def start(eng, m):
            return m * L if isinstance(m, int) else eng.snap(m * L)

        @block.tensor
        def _(pe):
            def fill(stage, m, name):
                u = uses(stage, m, name)
                if not (isinstance(u, int) and u == 1):
                    pe.wait_ge(drained[BANK[name]], u - 1)
                return work[BANK[name]]

            def prep(m, name):
                w = None
                tok0 = start(pe, m)
                if name == "dp":
                    if isinstance(m, int):
                        pe.wait_ge(x_in, 16 * (m + 1))
                    w = fill("prep", m, name)
                    for k in range(DT):
                        mm = nc.tensor.matmul(w[0:R, :], col("wp")[:, k * R:(k + 1) * R], xT[:, k, ds(tok0, L)],
                                              start=(k == 0), stop=(k == DT - 1))
                elif name in ("z0", "z1"):
                    w = fill("prep", m, name)
                    dt = int(name[1])
                    if dt == 0:
                        drain_of(pe, "prep", m, "dp")
                    mm = nc.tensor.matmul(w[:, :], wdt[:, dt * P:(dt + 1) * P], dps[:, :], start=True, stop=True)
                else:
                    w = fill("prep", m, name)
                    o = "BC".index(name) * DT * P
                    for k in range(DT):
                        mm = nc.tensor.matmul(w[:, :], col("wbc")[:, o + k * P:o + (k + 1) * P],
                                              xT[:, k, ds(tok0, L)], start=(k == 0), stop=(k == DT - 1))
                mm.then_inc(full[BANK[name]], 1)

            def expand(b, n, par, what):
                dt, q, k, c, j = geometry(n)
                ring, done, read = ((da, decay_in, scanned), (dxp, drive_in, bx_ready))[what]
                if not (isinstance(b, int) and NG * b + n < 2):
                    pe.wait_ge(read, NG * b + n - 1)
                nc.tensor.matmul(ring[n % 2][:, :], sel[:, j, :], hl_flat[what][:, ds(par * 4 * L + c * L, L)],
                                 start=True, stop=True).then_inc(done, 1)

            def sum_quad(b, k):
                pe.wait_ge(hc_ready, NG * b + 4 * k + 4)
                if k % 4 == 0 and not (isinstance(b, int) and b == 0 and k == 0):
                    pe.wait_ge(y_taken, DT * b + k // 4)
                for q in range(4):
                    mm = nc.tensor.matmul(yp[32 * q:32 * q + 32, :], col("ysel")[:, (k % 4) * 32:(k % 4) * 32 + 32],
                                          hc[:, (4 * k + q) % 8, :], start=(k % 4 == 0), stop=(k % 4 == 3))
                mm.then_inc(y_quads, 1)

            def post(m, name):
                if name in ("turn0", "turn1"):
                    i = int(name[4])
                    if i == 0:
                        pe.wait_ge(y_taken, DT * (m + 1))
                    w = fill("post", m, name)
                    for t in range(2):
                        for dt in range(DT):
                            mm = nc.tensor.transpose(w[:, t * D + dt * P:t * D + (dt + 1) * P],
                                                     rT[:, dt, (2 * i + t) * P:(2 * i + t + 1) * P], ident)
                    mm.then_inc(full[BANK[name]], 1)
                elif name in ("back0", "back1"):
                    dt = int(name[4])
                    if dt == 0:
                        drain_of(pe, "post", m, "turn1")
                    w = fill("post", m, name)
                    for t in range(TT):
                        mm = nc.tensor.transpose(w[:, t * P:(t + 1) * P], xn4[:, t, dt * P:(dt + 1) * P], ident)
                    mm.then_inc(full[BANK[name]], 1)
                elif name == "logits":
                    drain_of(pe, "post", m, "back1")
                    w = fill("post", m, name)
                    for t in range(TT):
                        terms = [(x, k) for x in (xhi, xlo) for k in range(DT)]
                        for i, (x, k) in enumerate(terms):
                            mm = nc.tensor.matmul(w[:, t * 2 * E:(t + 1) * 2 * E], x[:, k, t * P:(t + 1) * P],
                                                  rw[:, k, :, :].rearrange("p s e -> p (s e)"),
                                                  start=(i == 0), stop=(i == len(terms) - 1))
                    mm.then_inc(full[BANK[name]], 1)
                elif name == "ranks":
                    pe.wait_ge(picked, m + 1)
                    w = fill("post", m, name)
                    nc.tensor.matmul(w[:, 0:TT * E], lower[:, 0, :], oh_b[:, :, :].rearrange("p t e -> p (t e)"),
                                     start=True, stop=True)
                    nc.tensor.matmul(w[:, TT * E:2 * TT * E], lower[:, 1, :],
                                     oh_b[:, :, :].rearrange("p t e -> p (t e)"),
                                     start=True, stop=True).then_inc(full[BANK[name]], 1)
                elif name[0] in "gu":
                    i, side = int(name[1:]), "gu".index(name[0])
                    w = fill("post", m, name)
                    terms = [(a, x, k) for a, x in ((wg_hi, xhi), (wg_hi, xlo), (wg_lo, xhi)) for k in range(DT)]
                    for t, (a, x, k) in enumerate(terms):
                        mm = nc.tensor.matmul(w[:, :], a[:, side, k, i * P:(i + 1) * P], x[:, k, :],
                                              start=(t == 0), stop=(t == len(terms) - 1))
                    mm.then_inc(full[BANK[name]], 1)
                else:
                    i = int(name[4])
                    w = fill("post", m, name)
                    for t in range(2):
                        for k in range(NI):
                            if i == 0 and t == 0:
                                drain_of(pe, "post", m, f"u{k}")
                            mm = nc.tensor.matmul(w[:, t * D:(t + 1) * D],
                                                  act[:, k, (2 * i + t) * P:(2 * i + t + 1) * P], wd[:, k, :],
                                                  start=(k == 0), stop=(k == NI - 1))
                    mm.then_inc(full[BANK[name]], 1)

            def batch(b, with_prep, with_post):
                par = parity(pe, b)
                pe.wait_ge(moved, 128 * (b + 1))
                expand(b, 0, par, 1)
                for n in range(NG):
                    expand(b, n, par, 0)
                    if n + 1 < NG:
                        expand(b, n + 1, par, 1)
                    if n % 4 == 3 and n > 3:
                        sum_quad(b, n // 4 - 1)
                    if with_post and n == LAST_QUAD_AT:
                        sum_quad(b - 1, NQ - 1)
                    if with_prep and n in PREP_AT:
                        for name in PREP_AT[n]:
                            prep(b + 1, name)
                    if with_post and n in POST_AT:
                        for name in POST_AT[n]:
                            post(b - 1, name)

            pe.wait_ge(packed, 16)
            pe.wait_ge(wdt_in, 16)
            for name in PREP:
                prep(0, name)
            pe.wait_ge(const_ready, SCAN_ACT)
            batch(0, True, False)
            pe.wait_ge(const_ready, SETUP_ACT)
            pe.wait_ge(dconst, SETUP_DVE)
            pe.wait_ge(down_in, 16)
            with pe.Fori(1, NB - 1) as b:
                batch(b, True, True)
            batch(NB - 1, False, True)
            sum_quad(NB - 1, NQ - 1)
            for name in POST:
                post(NB - 1, name)

            w1_flat = w1[:, :, :, :].rearrange("p e k n -> p (e k n)")
            w2_flat = w2[:, :, :, :].rearrange("p e k n -> p (e k n)")

            def turn_rows(i, c):
                pe.wait_ge(rows_in[c % 4], 16 * i + 16 * (c // 4 + 1))
                if c >= 1:
                    pe.wait_ge(xbT_ready, 4 * i + c)
                for dt in range(DT):
                    mm = nc.tensor.transpose(xt_p[:, dt * P:(dt + 1) * P], xb[:, c % 4, dt * P:(dt + 1) * P], ident)
                mm.then_inc(xt_full, 1)

            def up(i, c):
                expert = pe.value_load(info[0:1, 0, ds(i * 4 + c, 1)], min_val=0, max_val=E - 1)
                base = pe.snap(expert * (DT * 2 * INTER))
                pe.wait_ge(w1_in, pe.snap(expert * 16 + 16))
                alone(pe)
                pe.wait_ge(xbT_ready, 4 * i + c + 1)
                if c >= 2:
                    pe.wait_ge(ab_ready, 4 * i + c - 1)
                for half, (dst, done) in enumerate(((gate_p, gate_full), (up_p, up_full))):
                    for k in range(DT):
                        mm = nc.tensor.matmul(dst[c % 2][:, :], xbT[:, c % 2, k, :],
                                              w1_flat[:, ds(base + (k * 2 + half) * INTER, INTER)],
                                              start=(k == 0), stop=(k == DT - 1))
                    mm.then_inc(done, 1)

            def turn_act(i, c):
                pe.wait_ge(ab_ready, 4 * i + c + 1)
                if c >= 1:
                    pe.wait_ge(aT_ready, 4 * i + c)
                for k in range(INTER // P):
                    mm = nc.tensor.transpose(at_p[:, k * P:(k + 1) * P], ab[:, c % 2, k * P:(k + 1) * P], ident)
                mm.then_inc(at_full, 1)

            def down(i, c):
                expert = pe.value_load(info[0:1, 0, ds(i * 4 + c, 1)], min_val=0, max_val=E - 1)
                base = pe.snap(expert * (INTER // P * D))
                pe.wait_ge(w2_in, pe.snap(expert * 16 + 16))
                alone(pe)
                pe.wait_ge(aT_ready, 4 * i + c + 1)
                if c >= 2:
                    pe.wait_ge(ob_ready, 4 * i + c - 1)
                for k in range(INTER // P):
                    mm = nc.tensor.matmul(out_p[c % 2][:, 0:D], aT[:, c % 2, k * P:(k + 1) * P],
                                          w2_flat[:, ds(base + k * D, D)], start=(k == 0), stop=(k == INTER // P - 1))
                mm.then_inc(out_full, 1)

            pe.wait_ge(info_ready, 1)
            turn_rows(0, 0)
            turn_rows(0, 1)
            up(0, 0)

            def step(i, c):
                if c + 2 < NBLK:
                    turn_rows(i, c + 2)
                if c + 1 < NBLK:
                    up(i, c + 1)
                if c >= 1:
                    down(i, c - 1)
                turn_act(i, c)

            blocks(pe, step)
            down(0, NBLK - 1)

        @block.scalar
        def _(se):
            act_ = nc.scalar.activation

            def prep(m, name):
                if name == "dp":
                    w = filled(se, "prep", m, name)
                    act_(dps[:, :], w[0:R, :], ACT.Copy).then_inc(drained[BANK[name]], 1)
                elif name in ("z0", "z1"):
                    dt = int(name[1])
                    if not (isinstance(m, int) and m == 0):
                        se.wait_ge(lo_ready, DT * m)
                    w = filled(se, "prep", m, name)
                    bias = col("bdt")[:, dt:dt + 1]
                    act_(lnt[:, dt, :], w[:, :], ACT.Abs, bias=bias)
                    act_(rel[:, dt, :], w[:, :], ACT.Relu, bias=bias).then_inc(drained[BANK[name]], 1)
                elif name == "log":
                    drain_of(se, "prep", m, "z1")
                    act_(lnt[:, :, :], lnt[:, :, :], ACT.Exp, scale=-1.0).then_inc(z_exp, 1)
                    se.wait_ge(z_exp, m + 1)
                    act_(lnt[:, :, :], lnt[:, :, :], ACT.Ln, bias=1.0).then_inc(z_log, 1)
                elif name in ("B", "C"):
                    w = filled(se, "prep", m, name)
                    if not (isinstance(m, int) and m < 2):
                        se.wait_ge(hc_ready, NG * (m - 1))
                    o = parity(se, m) * 2 * L + "BC".index(name) * L
                    act_(bc_flat[:, ds(o, L)], w[:, :], ACT.Copy).then_inc(drained[BANK[name]], 1)
                else:
                    i = int(name[2])
                    se.wait_ge((delta_ready, dx_ready)[i], m + 1)
                    if not (isinstance(m, int) and m == 0):
                        se.wait_ge(moved, 128 * m)
                    act_(hi[i][:, :, :], (rel, lnt)[i][:, :, :], ACT.Copy).then_inc(hi_ready, 1)

            def post(m, name):
                if name in ("turn0", "turn1"):
                    i = int(name[4])
                    se.wait_ge(rstd_ready, 2 * m + i + 1)
                    if i == 0:
                        se.wait_ge(xn_out, 16 * (m + 1))
                        se.wait_ge(sums_out, 16 * (m + 1))
                    w = filled(se, "post", m, name)
                    for t in range(2):
                        a = act_(xn4[:, 2 * i + t, :], w[:, t * D:(t + 1) * D], ACT.Identity,
                                 bias=nbias[:, 2 * i + t:2 * i + t + 1], scale=rstd[:, 2 * i + t:2 * i + t + 1])
                    a.then_inc(drained[BANK[name]], 1)
                elif name in ("back0", "back1"):
                    dt = int(name[4])
                    w = filled(se, "post", m, name)
                    act_(xhi[:, dt, :], w[:, :], ACT.Copy).then_inc(xhi_ready, 1)
                elif name == "ex":
                    se.wait_ge(picked, m + 1)
                    act_(ex[:, :], gap[:, :], ACT.Exp).then_inc(ex_ready, 1)
                else:
                    i = int(name[1:])
                    w = filled(se, "post", m, name)
                    act_(th[:, i % 2, :], w[:, :], ACT.Tanh, scale=0.5).then_inc(th_ready, 1)

            def batch(b, with_prep, with_post):
                for n in range(NG):
                    se.wait_ge(decay_in, NG * b + n + 1)
                    act_(da[n % 2][:, :], da[n % 2][:, :], ACT.Exp,
                         scale=aneg[:, n:n + 1]).then_inc(decay_ready, 1)
                    if with_prep:
                        for name in PREP_ACT.get(n, ()):
                            prep(b + 1, name)
                    if with_post:
                        for name in POST_ACT.get(n, ()):
                            post(b - 1, name)
                    elif n in SHARED_ACT:
                        side, k = divmod(SHARED_ACT[n], DT)
                        se.wait_ge(shared_in, 16)
                        act_(wg_hi[:, side, k, :], wg_raw[:, side, k, :], ACT.Copy).then_inc(const_ready, 1)

            se.wait_ge(packed, 16)
            act_(aneg[:, :], col("alog"), ACT.Exp).then_inc(const_ready, 1)
            act_(rw[:, :, 0, :], col("rw").rearrange("p (k e) -> p k e", e=E), ACT.Copy).then_inc(const_ready, 1)
            act_(lower[:, :, :].rearrange("p k e -> p (k e)"), col("lower"), ACT.Copy).then_inc(const_ready, 1)
            for name in ("dp", "z0", "z1", "log", "B", "C"):
                prep(0, name)
            se.wait_ge(sel_in, 16)
            act_(sel[:, :, :], sel_raw[:, :, :], ACT.Copy).then_inc(const_ready, 1)
            for name in ("hi0", "hi1"):
                prep(0, name)
            se.wait_ge(dconst, SCAN_DVE)
            batch(0, True, False)
            with se.Fori(1, NB - 1) as b:
                batch(b, True, True)
            batch(NB - 1, False, True)
            for n in range(NG):
                for name in POST_ACT.get(n, ()):
                    post(NB - 1, name)

            def rows(i, c):
                se.wait_ge(xt_full, 4 * i + c + 1)
                if c >= 2:
                    se.wait_ge(up_full, 4 * i + c - 1)
                act_(xbT[:, c % 2, :, :].rearrange("p k t -> p (k t)"), xt_p[:, 0:D], ACT.Copy).then_inc(xbT_ready, 1)

            def silu(i, c):
                se.wait_ge(gate_full, 4 * i + c + 1)
                if c >= 2:
                    se.wait_ge(ab_ready, 4 * i + c - 1)
                act_(sg[:, c % 2, :], gate_p[c % 2][:, :], ACT.Silu).then_inc(sg_ready, 1)

            def scale(i, c):
                se.wait_ge(out_full, 4 * i + c + 1)
                se.wait_ge(list_in[c % 4], 16 * i + 16 * (c // 4 + 1))
                if c >= 2:
                    se.wait_ge(added, 16 * (4 * i + c - 1))
                act_(ob[:, c % 2, :], out_p[c % 2][:, 0:D], ACT.Copy,
                     scale=lst[:, c % 4, 1:2].bitcast(F32)).then_inc(ob_ready, 1)

            rows(0, 0)
            rows(0, 1)
            silu(0, 0)

            def step(i, c):
                if c + 2 < NBLK:
                    rows(i, c + 2)
                if c + 1 < NBLK:
                    silu(i, c + 1)
                if c >= 1:
                    scale(i, c - 1)

            blocks(se, step)
            scale(0, NBLK - 1)
            for b in range(NB):
                se.wait_ge(fin_rstd, b + 1)
                for t in range(TT):
                    j = b * TT + t
                    a = act_(fin_o[:, b, t, :], fin[:, b, t, :], ACT.Identity,
                             bias=fin_nb[:, j:j + 1], scale=fin_rs[:, j:j + 1])
                a.then_inc(fin_ready, 1)

        @block.vector
        def _(ve_):
            tt = nc.vector.tensor_tensor
            chain = {"k": 0}

            def prep(m, name):
                if name == "delta":
                    ve_.wait_ge(z_log, m + 1)
                    tt(out=rel[:, :, :], in0=rel[:, :, :], in1=lnt[:, :, :], op=ALU.add).then_inc(delta_ready, 1)
                elif name == "dx":
                    t0 = start(ve_, m)
                    ve_.wait_ge(delta_ready, m + 1)
                    if isinstance(m, int):
                        ve_.wait_ge(x_in, 16 * (m + 1))
                    tt(out=lnt[:, :, :], in0=rel[:, :, :], in1=xT[:, :, ds(t0, L)], op=ALU.mult).then_inc(dx_ready, 1)
                else:
                    i = int(name[2])
                    ve_.wait_ge(hi_ready, DT * m + i + 1)
                    if i:
                        ve_.wait_ge(dx_ready, m + 1)
                    if not (isinstance(m, int) and m == 0):
                        ve_.wait_ge(moved, 128 * m)
                    tt(out=lo[i][:, :, :], in0=(rel, lnt)[i][:, :, :], in1=hi[i][:, :, :].bitcast(F32),
                       op=ALU.subtract).then_inc(lo_ready, 1)

            def drive(b, n, bo):
                ve_.wait_ge(drive_in, NG * b + n + 1)
                if n == 0:
                    wait_prepared(ve_, b, "B")
                if not (isinstance(b, int) and NG * b + n < 2):
                    ve_.wait_ge(scanned, NG * b + n - 1)
                tt(out=bx[:, n % 2, :], in0=dxp[n % 2][:, :], in1=bc_flat[:, ds(bo, L)],
                   op=ALU.mult).then_inc(bx_ready, 1)

            def scan(b, n):
                ve_.wait_ge(decay_ready, NG * b + n + 1)
                ve_.wait_ge(bx_ready, NG * b + n + 1)
                if not (isinstance(b, int) and NG * b + n < 4):
                    ve_.wait_ge(hc_ready, NG * b + n - 3)
                nc.vector.tensor_tensor_scan(out=h[:, n % 4, :], data0=da[n % 2][:, :], data1=bx[:, n % 2, :],
                                             initial=0.0, op0=ALU.mult, op1=ALU.add).then_inc(scanned, 1)

            def take_y(b, dt):
                t0 = start(ve_, b)
                ve_.wait_ge(y_quads, NQ * b + 4 * dt + 4)
                nc.vector.scalar_tensor_tensor(out=rT[:, dt, :], in0=xT[:, dt, ds(t0, L)], scalar=dp1[:, dt:dt + 1],
                                               in1=yp[:, :], op0=ALU.mult, op1=ALU.add).then_inc(y_taken, 1)

            def post(m, name):
                def link(instr):
                    chain["k"] += 1
                    instr.then_inc(rt_step, 1)
                    ve_.wait_ge(rt_step, RT_STEPS * m + chain["k"])

                def per_token(ap):
                    return ap.unsqueeze(2).to_broadcast([P, TT, E])

                def per_expert(ap):
                    return ap.unsqueeze(1).to_broadcast([P, TT, E])

                if name in ("turn0", "turn1"):
                    i = int(name[4])
                    w = filled(ve_, "post", m, name)
                    for t in range(2):
                        s = nc.vector.bn_stats(bn[:, 2 * i + t, :], w[:, t * D:(t + 1) * D])
                    s.then_inc(bn_step, 1)
                    ve_.wait_ge(bn_step, 2 * m + i + 1)
                    alone(ve_)
                    for t in range(2):
                        s = nc.vector.bn_aggr(mv[:, 2 * i + t, :], bn[:, 2 * i + t, :])
                    s.then_inc(stats, 1)
                elif name in ("back0", "back1"):
                    dt = int(name[4])
                    ve_.wait_ge(xhi_ready, DT * m + dt + 1)
                    w = filled(ve_, "post", m, name)
                    tt(out=xlo[:, dt, :], in0=w[:, :], in1=xhi[:, dt, :].bitcast(F32),
                       op=ALU.subtract).then_inc(drained[BANK[name]], 1)
                elif name == "logits":
                    chain["k"] = 0
                    w = filled(ve_, "post", m, name)
                    parts = w[:, 0:2 * TT * E].rearrange("p (t s e) -> p t s e", s=2, e=E)
                    link(nc.vector.tensor_copy(lg[:, :, :], parts[:, :, 0, :]))
                    tt(out=lg[:, :, :], in0=lg[:, :, :], in1=parts[:, :, 1, :],
                       op=ALU.add).then_inc(drained[BANK[name]], 1)
                elif name in ("first", "second"):
                    k = 1 if name == "second" else 0
                    src = (lg, lg2)[k]
                    if k == 0:
                        drain_of(ve_, "post", m, "logits")
                    link(nc.vector.tensor_reduce(out=mx[:, k, :], in_=src[:, :, :], axis=AX, op=ALU.max))
                    link(tt(out=eq[:, k], in0=src[:, :, :], in1=per_token(mx[:, k, :]), op=ALU.is_equal))
                    link(tt(out=key[:, k], in0=eq[:, k], in1=per_expert(rev), op=ALU.mult))
                    link(nc.vector.tensor_reduce(out=kk[:, k, :], in_=key[:, k], axis=AX, op=ALU.max))
                    link(tt(out=oh[:, k], in0=per_expert(rev), in1=per_token(kk[:, k, :]), op=ALU.is_equal))
                    if k == 0:
                        link(nc.vector.scalar_tensor_tensor(
                            out=lg2[:, :, :], in0=oh[:, 0], scalar=-3e38, in1=lg[:, :, :],
                            op0=ALU.mult, op1=ALU.add))
                    else:
                        link(tt(out=gap[:, :], in0=mx[:, 1, :], in1=mx[:, 0, :], op=ALU.subtract))
                        tt(out=oh_b[:, :, :], in0=oh[:, 0], in1=oh[:, 1], op=ALU.add).then_inc(picked, 1)
                elif name == "ex":
                    ve_.wait_ge(ex_ready, m + 1)
                    link(nc.vector.tensor_scalar_add(den[:, :], ex[:, :], 1.0))
                    link(nc.vector.reciprocal(sc[:, 0, :], den[:, :]))
                    link(tt(out=sc[:, 1, :], in0=ex[:, :], in1=sc[:, 0, :], op=ALU.mult))
                elif name == "ranks":
                    w = filled(ve_, "post", m, name)
                    tot = w[:, TT * E:2 * TT * E].rearrange("p (t e) -> p t e", e=E)
                    for t in range(TT):
                        link(tt(out=offs[:, t + 1, :], in0=offs[:, t, :], in1=tot[:, t, :], op=ALU.add))
                    tt(out=rk[:, :, :], in0=w[:, 0:TT * E].rearrange("p (t e) -> p t e", e=E),
                       in1=offs[:, 0:TT, :], op=ALU.add).then_inc(drained[BANK[name]], 1)
                    drain_of(ve_, "post", m, name)
                    link(nc.vector.tensor_copy(offs[:, 0, :], offs[:, TT, :]))
                    link(tt(out=rk2[:, :, :], in0=rk[:, :, :], in1=per_expert(region), op=ALU.add))
                elif name in ("rows0", "rows1"):
                    k = int(name[4])
                    t0 = m * TT if isinstance(m, int) else ve_.snap(m * TT)
                    link(tt(out=pr[:, k], in0=oh[:, k], in1=rk2[:, :, :], op=ALU.mult))
                    link(nc.vector.tensor_reduce(out=posf[:, k, :], in_=pr[:, k], axis=AX, op=ALU.add))
                    link(nc.vector.tensor_copy(ent[:, k, :, 1:2].bitcast(F32), sc[:, k, :].unsqueeze(2)))
                    alone(ve_)
                    link(nc.vector.tensor_copy(ent[:, k, :, 0:1], tok[:, ds(t0, TT)].unsqueeze(2)))
                    if k == 1:
                        assert chain["k"] == RT_STEPS, chain
                        nc.vector.tensor_copy(pos[:, :, :], posf[:, :, :]).then_inc(ent_ready, 1)
                elif name[0] == "g":
                    i = int(name[1:])
                    ve_.wait_ge(th_ready, NI * m + i + 1)
                    w = filled(ve_, "post", m, name)
                    nc.vector.scalar_tensor_tensor(out=act[:, i, :], in0=th[:, i % 2, :], scalar=1.0, in1=w[:, :],
                                                   op0=ALU.add, op1=ALU.mult).then_inc(drained[BANK[name]], 1)
                elif name[0] == "u":
                    i = int(name[1:])
                    drain_of(ve_, "post", m, f"g{i}")
                    w = filled(ve_, "post", m, name)
                    nc.vector.scalar_tensor_tensor(out=act[:, i, :], in0=act[:, i, :], scalar=0.5, in1=w[:, :],
                                                   op0=ALU.mult, op1=ALU.mult).then_inc(drained[BANK[name]], 1)
                else:
                    i = int(name[4])
                    ve_.wait_ge(xn_out, 16 * (m + 2))
                    w = filled(ve_, "post", m, name)
                    o = xn4[:, 2 * i:2 * i + 2, :].rearrange("p t d -> p (t d)")
                    tt(out=o, in0=w[:, :], in1=o, op=ALU.add).then_inc(drained[BANK[name]], 1)

            def batch(b, with_prep, with_post):
                bo = parity(ve_, b) * 2 * L
                if not isinstance(bo, int):
                    bo = ve_.snap(bo)
                drive(b, 0, bo)
                for n in range(NG):
                    if n + 1 < NG:
                        drive(b, n + 1, bo)
                    scan(b, n)
                    if with_post and n == Y1_AT:
                        take_y(b - 1, 1)
                    if n == Y0_AT:
                        take_y(b, 0)
                    if with_prep:
                        for name in PREP_DVE.get(n, ()):
                            prep(b + 1, name)
                    if with_post:
                        for name in POST_DVE.get(n, ()):
                            post(b - 1, name)
                    elif n in SHARED_DVE:
                        side, k = divmod(SHARED_DVE[n], DT)
                        ve_.wait_ge(const_ready, SCAN_ACT + SHARED_DVE[n] + 1)
                        tt(out=wg_lo[:, side, k, :], in0=wg_raw[:, side, k, :],
                           in1=wg_hi[:, side, k, :].bitcast(F32), op=ALU.subtract).then_inc(dconst, 1)

            nc.vector.memset(mhalf[:, :], -0.5).then_inc(dconst, 1)
            nc.vector.memset(offs[:, 0, :], 0.0).then_inc(dconst, 1)
            nc.vector.memset(xn4[:, 0, :], 0.0).then_inc(dconst, 1)
            ve_.wait_ge(packed, 16)
            nc.vector.tensor_scalar_add(dp1[:, :], col("dpar"), 1.0).then_inc(dconst, 1)
            ve_.wait_ge(const_ready, 2)
            nc.vector.tensor_scalar_mul(aneg[:, :], aneg[:, :], -1.0).then_inc(dconst, 1)
            tt(out=rw[:, :, 1, :], in0=col("rw").rearrange("p (k e) -> p k e", e=E),
               in1=rw[:, :, 0, :].bitcast(F32), op=ALU.subtract).then_inc(dconst, 1)
            for name in ("delta", "dx", "lo0", "lo1"):
                prep(0, name)
            ve_.wait_ge(dconst, SCAN_DVE)
            batch(0, True, False)
            ve_.wait_ge(dconst, SETUP_DVE)
            with ve_.Fori(1, NB - 1) as b:
                batch(b, True, True)
            batch(NB - 1, False, True)
            take_y(NB - 1, 1)
            for n in range(NG):
                for name in POST_DVE.get(n, ()):
                    if not name.startswith("down"):
                        post(NB - 1, name)

            blk = {"k": 0}

            def link(instr):
                blk["k"] += 1
                instr.then_inc(info_step, 1)
                ve_.wait_ge(info_step, blk["k"])

            def by_expert(ap):
                return ap.unsqueeze(1).to_broadcast([1, NBLK, E])

            def by_block(ap):
                return ap.unsqueeze(2).to_broadcast([1, NBLK, E])

            number, expert = col("block", 1), col("expert", 1)
            link(nc.vector.tensor_scalar_add(cnti[:, 0, :], offs[0:1, 0, :], float(P - 1)))
            link(nc.vector.tensor_single_scalar(cnti[:, 1, :], cnti[:, 0, :], 7, op=ALU.arith_shift_right))
            link(nc.vector.tensor_copy(cnt[:, 0, :], cnti[:, 1, :]))
            link(nc.vector.memset(cnt[:, 1, :], 1.0))
            link(nc.vector.tensor_tensor_scan(out=cnt[:, 2, :], data0=cnt[:, 1, :], data1=cnt[:, 0, :],
                                              initial=0.0, op0=ALU.mult, op1=ALU.add))
            link(tt(out=cnt[:, 3, :], in0=cnt[:, 2, :], in1=cnt[:, 0, :], op=ALU.subtract))
            link(tt(out=btw[:, :, :], in0=by_block(number), in1=by_expert(cnt[:, 2, :]), op=ALU.is_ge))
            link(nc.vector.tensor_reduce(out=btc[:, 0, :], in_=btw[:, :, :], axis=AX, op=ALU.add))
            link(nc.vector.tensor_scalar(out=btc[:, 1, :], in0=btc[:, 0, :], scalar1=float(E), scalar2=None,
                                         op0=ALU.is_lt))
            link(nc.vector.tensor_scalar(out=btc[:, 2, :], in0=btc[:, 0, :], scalar1=float(E - 1), scalar2=None,
                                         op0=ALU.min))
            link(tt(out=btw[:, :, :], in0=by_expert(expert), in1=by_block(btc[:, 2, :]), op=ALU.is_equal))
            link(tt(out=btw[:, :, :], in0=btw[:, :, :], in1=by_expert(cnt[:, 3, :]), op=ALU.mult))
            link(nc.vector.tensor_reduce(out=btc[:, 3, :], in_=btw[:, :, :], axis=AX, op=ALU.add))
            link(tt(out=btc[:, 4, :], in0=number, in1=btc[:, 3, :], op=ALU.subtract))
            link(nc.vector.tensor_scalar(out=btc[:, 5, :], in0=btc[:, 4, :], scalar1=float(P),
                                         scalar2=-float(E * REGION), op0=ALU.mult, op1=ALU.add))
            link(nc.vector.scalar_tensor_tensor(out=btc[:, 6, :], in0=btc[:, 2, :], scalar=float(REGION),
                                                in1=btc[:, 5, :], op0=ALU.mult, op1=ALU.add))
            link(tt(out=btc[:, 7, :], in0=btc[:, 6, :], in1=btc[:, 1, :], op=ALU.mult))
            link(nc.vector.tensor_copy(info[:, 0, :], btc[:, 2, :]))
            nc.vector.tensor_scalar_add(info[:, 1, :], btc[:, 7, :], float(E * REGION)).then_inc(info_ready, 1)
            for name in ("down0", "down1"):
                post(NB - 1, name)

            def gated(i, c):
                ve_.wait_ge(sg_ready, 4 * i + c + 1)
                ve_.wait_ge(up_full, 4 * i + c + 1)
                if c >= 2:
                    ve_.wait_ge(at_full, 4 * i + c - 1)
                tt(out=ab[:, c % 2, :], in0=up_p[c % 2][:, :], in1=sg[:, c % 2, :], op=ALU.mult).then_inc(ab_ready, 1)

            def turned(i, c):
                ve_.wait_ge(at_full, 4 * i + c + 1)
                if c >= 2:
                    ve_.wait_ge(out_full, 4 * i + c - 1)
                nc.vector.tensor_copy(aT[:, c % 2, :], at_p[:, :]).then_inc(aT_ready, 1)

            gated(0, 0)

            def step(i, c):
                if c + 1 < NBLK:
                    gated(i, c + 1)
                turned(i, c)

            blocks(ve_, step)
            for b in range(NB):
                ve_.wait_ge(fin_in[b], 16)
                for t in range(TT):
                    s = nc.vector.bn_stats(fin_bn[:, b * TT + t, :], fin[:, b, t, :])
                s.then_inc(bn_step, 1)
                ve_.wait_ge(bn_step, 2 * NB + b + 1)
                for t in range(TT):
                    s = nc.vector.bn_aggr(fin_mv[:, b * TT + t, :], fin_bn[:, b * TT + t, :])
                s.then_inc(stats, 1)

        @block.gpsimd
        def _(po):
            def rstd_of(lo_, hi_, done, k, buffers):
                r = slice(lo_, hi_)
                mv, ve, mhalf, rstd, nbias = buffers
                var, mean = mv[:, r, 1:2].squeeze(2), mv[:, r, 0:1].squeeze(2)
                alone(po)
                po.tensor_scalar(out=ve[:, r], in0=var, scalar1=EPS, scalar2=None, op0=ALU.add).then_inc(rs_step, 1)
                own = 1 if mv is fin_mv else 0
                po.wait_ge(rs_step, 2 * k + 1 + own)
                po.tensor_tensor(out=rstd[:, r], in0=ve[:, r], in1=mhalf[:, r], op=ALU.pow)
                po.tensor_scalar(out=nbias[:, r], in0=mean, scalar1=-1.0, scalar2=None, op0=ALU.mult).then_inc(rs_step, 1)
                po.wait_ge(rs_step, 2 * k + 2 + own)
                alone(po)
                po.tensor_tensor(out=nbias[:, r], in0=nbias[:, r], in1=rstd[:, r], op=ALU.mult).then_inc(done, 1)

            def post(m, name):
                if name in ("turn0", "turn1"):
                    i = int(name[4])
                    po.wait_ge(stats, 2 * m + i + 1)
                    rstd_of(2 * i, 2 * i + 2, rstd_ready, 2 * m + i, (mv, ve, mhalf, rstd, nbias))
                elif name == "landed":
                    po.wait_ge(scattered, 128 * (m + 1))
                    alone(po)
                else:
                    k, t = divmod(int(name[7:]), TT)
                    po.wait_ge(ent_ready, m + 1)
                    alone(po)
                    po.indirect_dma_start(out=list_d, in_=ent[:, k, t, :], in_offset=None,
                                          out_offset=bass.IndirectOffsetOnAxis(ap=pos[:, k, t:t + 1], axis=0)
                                          ).then_inc(scattered, 16)

            def batch(b, with_post):
                co = parity(po, b) * 2 * L + L
                if not isinstance(co, int):
                    co = po.snap(co)
                for n in range(NG):
                    po.wait_ge(scanned, NG * b + n + 1)
                    if n == 0:
                        wait_prepared(po, b, "C")
                    if not (isinstance(b, int) and NG * b + n < 8):
                        po.wait_ge(y_quads, NQ * b + (n - 8) // 4 + 1)
                    alone(po)
                    po.tensor_tensor(out=hc[:, n % 8, :], in0=h[:, n % 4, :], in1=bc_flat[:, ds(co, L)],
                                     op=ALU.mult).then_inc(hc_ready, 1)
                    if with_post:
                        for name in POST_POOL.get(n, ()):
                            post(b - 1, name)

            po.wait_ge(dconst, 3)
            batch(0, False)
            po.wait_ge(padded, 16)
            with po.Fori(1, NB - 1) as b:
                batch(b, True)
            batch(NB - 1, True)
            for n in range(NG):
                for name in POST_POOL.get(n, ()):
                    post(NB - 1, name)

            def gather(i, c):
                po.wait_ge(row_list_in[c % 4], 16 * i + 16 * (c // 4 + 1))
                if c >= 4:
                    po.wait_ge(xt_full, 4 * i + c - 3)
                alone(po)
                po.indirect_dma_start(out=xb[:, c % 4, :], out_offset=None, in_=xn_d,
                                      in_offset=bass.IndirectOffsetOnAxis(ap=lst_rows[:, c % 4, 0:1], axis=0)
                                      ).then_inc(rows_in[c % 4], 16)

            def add(i, c):
                po.wait_ge(ob_ready, 4 * i + c + 1)
                if c >= 1:
                    po.wait_ge(added, 16 * (4 * i + c))
                alone(po)
                po.indirect_dma_start(out=acc_d, in_=ob[:, c % 2, :], in_offset=None, compute_op=ALU.add,
                                      out_offset=bass.IndirectOffsetOnAxis(ap=lst[:, c % 4, 0:1], axis=0)
                                      ).then_inc(added, 16)

            po.wait_ge(xn_out, 16 * (NB + 1))
            for c in range(4):
                gather(0, c)
            po.wait_ge(sums_out, 16 * (NB + 1))

            def step(i, c):
                if c + 4 < NBLK:
                    gather(i, c + 4)
                if c >= 1:
                    add(i, c - 1)

            blocks(po, step)
            add(0, NBLK - 1)
            po.memset(fin_half[:, :], -0.5).then_inc(rs_step, 1)
            for b in range(NB):
                po.wait_ge(stats, 2 * NB + b + 1)
                rstd_of(b * TT, (b + 1) * TT, fin_rstd, 2 * NB + b, (fin_mv, fin_ve, fin_half, fin_rs, fin_nb))

        @block.sync
        def _(sp):
            sp.dma_start(pk[:, :], A["pack"]).then_inc(packed, 16)
            sp.dma_start(xT[:, :, 0:L], A["xT"][:, :, 0:L]).then_inc(x_in, 16)
            sp.dma_start(wdt[:, :], A["wdt"]).then_inc(wdt_in, 16)
            sp.dma_start(sel_raw[:, :, :], A["sel"]).then_inc(sel_in, 16)
            sp.dma_start(tok[:, :], A["tok"]).then_inc(tok_in, 16)

            def moves(m):
                par = parity(sp, m)
                sp.wait_ge(lo_ready, DT * (m + 1))
                alone(sp)
                if not (isinstance(m, int) and m < 2):
                    sp.wait_ge(drive_in, NG * (m - 1))
                    alone(sp)
                for i in range(2):
                    for side, src in ((0, hi[i]), (1, lo[i])):
                        for up_ in range(2):
                            to = slice(64 * (up_ ^ side), 64 * (up_ ^ side) + 64)
                            dst = hl[i][to, ds(par, 1), up_::2, :].rearrange("p a c l -> p (a c) l")
                            sp.dma_start(dst.bitcast(F32), src[64 * up_:64 * up_ + 64, :, :].bitcast(F32)
                                         ).then_inc(moved, 16)

            def rows_of(table, m):
                return table[ds(start(sp, m), L), :].rearrange("(t p) d -> p t d", p=P)

            def store(m, name):
                dst = rows_of((xn_d, acc_d)[name == "down1"], m)
                drain_of(sp, "post", m, name)
                alone(sp)
                sp.dma_start(dst, xn4[:, :, :]).then_inc((xn_out, sums_out)[name == "down1"], 16)

            moves(0)
            for b in range(1, NB):
                sp.wait_ge(x_in, 16 * b)
                sp.dma_start(xT[:, :, b * L:(b + 1) * L], A["xT"][:, :, b * L:(b + 1) * L]).then_inc(x_in, 16)
            sp.dma_start(wg_raw[:, :, :, :], A["wgu"]).then_inc(shared_in, 16)
            sp.dma_start(list_d, A["list"]).then_inc(padded, 16)
            sp.wait_ge(dconst, 3)
            sp.dma_start(xn_d[T:T + P, :], xn4[:, 0, :]).then_inc(xn_out, 16)
            sp.dma_start(acc_d[T:T + P, :], xn4[:, 0, :]).then_inc(sums_out, 16)
            sp.dma_start(wd[:, :, :], A["wd"]).then_inc(down_in, 16)
            moves(1)
            with sp.Fori(1, NB - 1) as b:
                store(b - 1, "turn1")
                moves(b + 1)
                store(b - 1, "down1")
            for name in ("turn1", "down1"):
                store(NB - 2, name)

            def load_expert(e):
                if e:
                    sp.wait_ge(w1_in, 16 * e)
                sp.dma_start(w1[:, e, :, :], A["w1"][:, e, :, :]).then_inc(w1_in, 16)
                if e:
                    sp.wait_ge(w2_in, 16 * e)
                sp.dma_start(w2[:, e, :, :], A["w2"][:, e, :, :]).then_inc(w2_in, 16)

            def list_row(i, c):
                return sp.value_load(info[0:1, 1, ds(i * 4 + c, 1)], min_val=0, max_val=NLIST - P)

            def fetch_rows(i, c):
                row = list_row(i, c)
                if c >= 4:
                    sp.wait_ge(rows_in[c % 4], 16 * i + 16 * (c // 4))
                    alone(sp)
                sp.dma_start(lst_rows[:, c % 4, :], list_d[ds(row, P), :]).then_inc(row_list_in[c % 4], 16)

            def fetch(i, c):
                row = list_row(i, c)
                if c >= 4:
                    sp.wait_ge(added, 16 * (4 * i + c - 3))
                    alone(sp)
                sp.dma_start(lst[:, c % 4, :], list_d[ds(row, P), :]).then_inc(list_in[c % 4], 16)

            sp.wait_ge(y_taken, DT * NB)
            load_expert(0)
            store(NB - 1, "turn1")
            for e in range(1, E):
                load_expert(e)
            sp.wait_ge(info_ready, 1)
            sp.wait_ge(scattered, 128 * NB)
            for c in range(4):
                fetch_rows(0, c)
            for c in range(4):
                fetch(0, c)
            store(NB - 1, "down1")
            fetch_rows(0, 4)

            def step(i, c):
                if c + 5 < NBLK:
                    fetch_rows(i, c + 5)
                if c >= 1 and c + 3 < NBLK:
                    fetch(i, c + 3)

            blocks(sp, step)
            sp.wait_ge(added, 16 * NBLK)
            for b in range(NB):
                sp.dma_start(fin[:, b, :, :],
                             acc_d[b * L:(b + 1) * L, :].rearrange("(t p) d -> p t d", p=P)).then_inc(fin_in[b], 16)
            for b in range(NB):
                sp.wait_ge(fin_ready, b + 1)
                sp.dma_start(out[b * L:(b + 1) * L, :].rearrange("(t p) d -> p t d", p=P),
                             fin_o[:, b, :, :]).then_inc(fin_out, 16)
            sp.wait_ge(fin_out, 16 * NB)


def kernel(**inputs):
    import concourse.bacc as _bacc
    from concourse.bass_utils import run_bass_kernel_spmd as _run

    x = np.asarray(inputs["L0_attn_x"])
    w_x, w_dt = np.asarray(inputs["L0_attn_W_x"]), np.asarray(inputs["L0_attn_W_dt"])

    def tiles(a):
        return np.ascontiguousarray(a.reshape(-1, P, a.shape[-1]).transpose(1, 0, 2))

    def bc_rows(a):
        return tiles(np.repeat(a.T, GC, axis=1)).reshape(P, DT * P)

    a_log = np.asarray(inputs["L0_attn_A_log"]).reshape(DT, 4, 4, GC, NS).transpose(4, 3, 0, 2, 1).reshape(P, NG)
    parts = {
        "wp": tiles(w_x[:R].T).reshape(P, -1),
        "wbc": np.concatenate([bc_rows(w_x[R:R + NS]), bc_rows(w_x[R + NS:])], axis=1),
        "bdt": np.asarray(inputs["L0_attn_b_dt"]).reshape(DT, P).T,
        "dpar": np.asarray(inputs["L0_attn_D"]).reshape(DT, P).T,
        "alog": a_log,
        "rw": tiles(np.asarray(inputs["L0_ffn_router_w"])).reshape(P, -1),
    }
    row = np.arange(P)
    state, chan = row // GC, row % GC
    ysel = np.zeros((P, 4, 32), np.float32)
    for k in range(4):
        ysel[row, k, GC * k + chan] = 1
    sel = np.zeros((P, 8, P), np.float32)
    for j in range(8):
        sel[:, j, :] = (row[:, None] % 64) == (GC * j + chan)[None, :]
    parts["ysel"] = ysel.reshape(P, -1)
    parts["ident"] = np.eye(P, dtype=np.float32)
    parts["lower"] = np.concatenate([np.triu(np.ones((P, P), np.float32), 1), np.ones((P, P), np.float32)], axis=1)
    for name, v in (("rev", E - np.arange(E)), ("region", REGION * np.arange(E)), ("expert", np.arange(E)),
                    ("block", np.arange(NBLK))):
        parts[name] = np.tile(v.astype(np.float32), (P, 1))
    slots = np.zeros((NLIST, 2), np.int32)
    slots[:, 0] = TRASH + np.arange(NLIST) % P
    arrays = {
        "pack": np.ascontiguousarray(np.concatenate([parts[n] for n, _ in PACK], axis=1)),
        "xT": tiles(x.reshape(T, D).T),
        "wdt": np.ascontiguousarray(w_dt.T),
        "sel": sel,
        "wgu": np.ascontiguousarray(np.stack([tiles(np.asarray(inputs["L0_ffn_w_gate"])),
                                              tiles(np.asarray(inputs["L0_ffn_w_up"]))], axis=1)),
        "wd": tiles(np.asarray(inputs["L0_ffn_w_down"])),
        "w1": np.ascontiguousarray(np.asarray(inputs["L0_ffn_w1"]).reshape(E, DT, P, 2 * INTER).transpose(2, 0, 1, 3)),
        "w2": np.ascontiguousarray(np.asarray(inputs["L0_ffn_w2"]).reshape(E, INTER // P, P, D).transpose(2, 0, 1, 3)),
        "tok": np.ascontiguousarray((row[:, None] + P * np.arange(T // P)[None, :]).astype(np.int32)),
        "list": slots,
    }
    nc = _bacc.Bacc("TRN2", target_bir_lowering=False, num_devices=1)
    args = {n: nc.dram_tensor(f"in_{n}", a.shape, mybir.dt.from_np(a.dtype), kind="ExternalInput").ap()
            for n, a in arrays.items()}
    out = nc.dram_tensor("out", (T, D), F32, kind="ExternalOutput").ap()
    program(nc, args, out)
    r = _run(nc, [{f"in_{n}": a for n, a in arrays.items()}], core_ids=[0])
    return r.results[0]["out"].reshape(x.shape)
```

```python
from contextlib import ExitStack

import numpy as np
import concourse.bass as bass
from concourse import mybir

P = 128
NB = 4
L = 512
T = NB * L
D = 256
DT = D // P
NS = 16
GC = P // NS
NG = D // GC
NQ = NG // 4
R = 64
XR = R + 2 * NS
TT = L // P
E = 8
INTER = 512
SI = 1024
NI = SI // P
NBLK = (2 * T) // P + E - 1
REGION = T
NLIST = E * REGION + P
TRASH = T
EPS = 1e-5

F32 = mybir.dt.float32
F32R = mybir.dt.float32r
BF16 = mybir.dt.bfloat16
I32 = mybir.dt.int32
ACT = mybir.ActivationFunctionType
ALU = mybir.AluOpType
AX = mybir.AxisListType.X
ds = bass.ds

PREP = ["dp", "z0", "z1", "B", "C"]
DOWN = ["down0", "down1"]
TURN = ["turn0", "turn1"]
BESIDE = (["dp", "z0", "z1", "back0", "back1", "logits", "g0", "u0", "B", "tokens", "g1", "u1", "C", "g2", "u2",
           "g3", "u3", "ranks"] + [f"{w}{i}" for i in range(4, NI) for w in "gu"])
MIDDLE = [n for n in BESIDE if n not in PREP]
ORDER = BESIDE + DOWN + TURN
BANK = {n: k % 3 for k, n in enumerate(BESIDE)} | {"down0": 1, "down1": 0, "turn0": 2, "turn1": 1}
FIRST, SECOND = range(0, 9), range(9, NG)

TENSOR_AT = {0: ["down0.0"], 2: ["down0.1"], 3: ["down0.2"], 4: ["down0.3"], 5: ["down1.0"],
             6: ["down1.1", "turn0", "turn1"], 7: ["down1.2"], 8: ["down1.3"], 10: ["dp"], 11: ["z0", "z1"],
             13: ["back0", "back1"], 14: ["logits"], 17: ["g0", "u0", "B"], 18: ["tokens", "g1"], 19: ["u1"],
             20: ["C"], 21: ["g2"], 22: ["u2", "g3"], 23: ["u3", "ranks"], 25: ["g4"], 26: ["u4"], 27: ["g5"],
             28: ["u5"], 29: ["g6", "u6"], 31: ["g7", "u7"]}
SCALAR_AT = {8: ["turn0"], 10: ["turn1", "dp"], 11: ["z0", "z1"], 13: ["back0", "back1"], 15: ["log"],
             17: ["logits", "g0"], 18: ["B", "hi0"], 19: ["g1"], 20: ["hi1"], 21: ["C"], 22: ["g2", "ex"],
             23: ["g3"], 27: ["g4", "g5"], 29: ["g6"], 31: ["g7"]}
VECTOR_AT = {4: ["down0"], 6: ["turn0", "turn1"], 8: ["down1"], 12: ["back0", "back1"], 15: ["delta"],
             17: ["u0", "dx", "tokens"], 18: ["first"], 19: ["u1"], 22: ["second", "u2"], 23: ["ex"], 24: ["u3"],
             25: ["ranks"], 26: ["u4"], 28: ["rows0"], 29: ["u5"], 31: ["rows1", "u6", "u7"]}
POOL_AT = {0: ["scatter0", "scatter1"], 2: ["scatter2", "scatter3", "scatter4"], 3: ["scatter5"], 4: ["scatter6"],
           5: ["scatter7", "turn0"], 6: ["turn1"], 8: ["landed"], 18: ["g0"], 21: ["lo0", "lo1"], 23: ["g2"],
           27: ["g4"], 31: ["g6"]}
SHARED_ACT = {22: 0, 24: 1, 26: 2, 28: 3}
SHARED_DVE = {23: 0, 25: 1, 27: 2, 29: 3}
LAST_QUAD_AT = 2
Y1_AT, Y0_AT = 2, 22
RT_STEPS = 30
PREP_STEPS = PREP + ["log", "delta", "dx", "hi0", "hi1", "lo0", "lo1"]


def side_steps(table, b, n):
    for name in table.get(n, ()):
        late = name.startswith(("down", "scatter")) or name == "landed"
        m = b + (1 if name in PREP_STEPS else -2 if late else -1)
        if not isinstance(b, int) or 0 <= m < NB:
            yield m, name


def last_post(table):
    return [(n, name) for n in SECOND for name in table.get(n, ())
            if name not in PREP_STEPS and name not in TURN]


W1_EARLY = 8
SPLIT_AT = {"g4": [4], "g5": [5], "g6": [6], "g7": [7]}
SPLIT_AFTER = {"u4": [4], "u5": [5], "u6": [6], "u7": [7]}
W1_FREE = {8: "u7", 12: "down1"}
SCAN_ACT, SETUP_ACT, SCAN_DVE, SETUP_DVE = 4, 8, 6, 10


def in_bank(k, names):
    return sum(BANK[n] == k for n in names)


def uses(m, name):
    k = BANK[name]
    u = m + (-1 if name in PREP else 0 if name in TURN else 1)
    inside = not isinstance(u, int)
    prep, middle, turn = in_bank(k, PREP), in_bank(k, MIDDLE + DOWN), in_bank(k, TURN)
    if inside:
        before, there = (u + 1) * prep + (u - 1) * middle + u * turn, ORDER
    else:
        before = min(u + 1, NB) * prep + max(u - 1, 0) * middle + min(max(u, 0), NB) * turn
        there = ((PREP if u < NB - 1 else []) + (MIDDLE + DOWN if u > 0 else []) + (TURN if 0 <= u < NB else []))
    return before + in_bank(k, [n for n in ORDER[:ORDER.index(name)] if n in there]) + 1


PACK = [("wp", DT * XR), ("bcsel", 2 * P), ("bdt", DT), ("dpar", DT), ("alog", NG), ("ysel", 4 * 32),
        ("ident", P), ("lower", 2 * P), ("rw", DT * E), ("rev", E), ("region", E), ("expert", E), ("block", NBLK)]
COL = {}
for _name, _n in PACK:
    COL[_name] = (sum(n for _, n in COL.values()) if COL else 0, _n)
NPACK = sum(n for _, n in PACK)


def program(nc, A, out):
    xn_d = nc.dram_tensor("xn_rows", [T + P, D], F32).ap()
    acc_d = nc.dram_tensor("acc_rows", [T + P, D], F32).ap()
    list_d = nc.dram_tensor("slot_list", [NLIST, 2], I32).ap()

    with ExitStack() as ctx:
        top = [(nc.sbuf_base + 63) // 64 * 64]

        def at(name, shape, dt=F32, offset=None):
            size = int(np.prod(shape[1:])) * (2 if dt == BF16 else 4)
            if offset is None:
                offset = top[0]
                top[0] += (size + 31) // 32 * 32
            return nc.alloc_sbuf_tensor_at(name, shape, dt, offset=offset)

        def sem(name):
            return ctx.enter_context(nc.semaphore(name))

        pk = at("pack", [P, NPACK])

        def col(name, rows=P):
            o, n = COL[name]
            return pk[0:rows, o:o + n]

        ident = col("ident")
        rev, region = col("rev"), col("region")
        lower = at("lower", [P, 2, P], BF16)
        tok = at("tok", [P, T // P], I32)
        bn = at("bn", [P, TT, 6])
        mv = at("mv", [P, TT, 2])
        ve = at("ve", [P, TT])
        mhalf = at("mhalf", [P, TT])
        rstd = at("rstd", [P, TT])
        nbias = at("nbias", [P, TT])
        offs = at("offs", [P, TT + 1, E])
        lst_rows = at("lst_rows", [P, 4, 2], I32)
        lst = at("lst", [P, 4, 2], I32)
        lg = at("lg", [P, TT, E])
        lg2 = at("lg2", [P, TT, E])
        eq = at("eq", [P, 2, TT, E])
        key = at("key", [P, 2, TT, E])
        oh = at("oh", [P, 2, TT, E])
        oh_b = at("oh_b", [P, TT, E], BF16)
        rk = at("rk", [P, TT, E])
        rk2 = at("rk2", [P, TT, E])
        pr = at("pr", [P, 2, TT, E])
        mx = at("mx", [P, 2, TT])
        kk = at("kk", [P, 2, TT])
        gap = at("gap", [P, TT])
        ex = at("ex", [P, TT])
        den = at("den", [P, TT])
        sc = at("sc", [P, 2, TT])
        posf = at("posf", [P, 2, TT])
        pos = at("pos", [P, 2, TT], I32)
        ent = at("ent", [P, 2, TT, 2], I32)
        rw = at("rw", [P, DT, 2, E], F32R)
        cnt = at("cnt", [1, 5, E])
        cnti = at("cnti", [1, 2, E], I32)
        btw_offset = top[0]
        btw = at("btw", [1, NBLK, E])
        btc = at("btc", [1, 8, NBLK])
        info = at("info", [1, 2, NBLK], I32)
        lgt = at("lgt", [2 * E, L], F32, btw_offset)
        rT_offset = top[0]
        rT = at("rT", [P, DT, L])
        xn4 = at("xn4", [P, TT, D])
        xhi = at("xhi", [P, DT, L], F32R)
        xlo = at("xlo", [P, DT, L], F32R)
        wd = at("wd", [P, NI, D])
        th_offset = top[0]
        th = at("th", [P, 2, L])
        gh = at("gh", [P, 2, L])
        act_offset = top[0]
        act = at("act", [P, NI, L])
        wg_hi = at("wg_hi", [P, 2, DT, SI], F32R)
        wg_lo = at("wg_lo", [P, 2, DT, SI], F32R)
        sel_raw = at("sel_raw", [P, 8, P], F32, th_offset)
        wg_raw = at("wg_raw", [P, 2, DT, SI], F32, act_offset)
        epoch = top[0]
        xT = at("xT", [P, DT, T])
        hl = [at("hl_delta", [P, 2, 4, L], F32R), at("hl_dx", [P, 2, 4, L], F32R)]
        bc = at("bc", [P, 2, 2, L])
        rel = at("rel", [P, DT, L])
        lnt = at("lnt", [P, DT, L])
        hi = [at("hi_delta", [P, DT, L], F32R), at("hi_dx", [P, DT, L], F32R)]
        lo = [at("lo_delta", [P, DT, L], F32R), at("lo_dx", [P, DT, L], F32R)]
        dps = at("dps", [XR, L])
        bx = at("bx", [P, 2, L])
        h = at("h", [P, 4, L])
        hc = at("hc", [P, 8, L])
        sel = at("sel", [P, 8, P], F32R)
        wdt = at("wdt", [R, D])
        aneg = at("aneg", [P, NG])
        dp1 = at("dp1", [P, DT])
        end_scan = top[0]
        assert end_scan <= nc.sbuf_usable_end, (end_scan, nc.sbuf_usable_end)
        w1_bytes = 2 * DT * 2 * INTER * 4
        w1_offset = epoch - E // 2 * w1_bytes
        assert w1_offset == th_offset - NI * D * 4
        w1 = at("w1", [P, E, 2, DT, 2 * INTER], F32R, w1_offset)
        top[0] = epoch + E // 2 * w1_bytes
        w2 = at("w2", [P, E, INTER // P, D])
        w1_raw = at("w1_raw", [P, 3, 2 * INTER])
        ab_offset = top[0]
        ab = at("ab", [P, 2, INTER])
        ob = at("ob", [P, 2, D])
        assert top[0] <= nc.sbuf_usable_end
        xb = at("xb", [P, 4, D], F32, rT_offset)
        sg = at("sg", [P, 2, INTER], F32, rT_offset + 4 * D * 4)
        xbT = at("xbT", [P, 2, 2, DT, P], F32R, rT_offset + 8 * D * 4)
        aT = at("aT", [P, 2, INTER], F32, rT_offset + 12 * D * 4)
        top[0] = w1_offset
        fin = at("fin", [P, NB, TT, D])
        fin_o = at("fin_o", [P, NB, TT, D])
        fin_bn = at("fin_bn", [P, NB * TT, 6])
        fin_mv = at("fin_mv", [P, NB * TT, 2])
        fin_ve = at("fin_ve", [P, NB * TT])
        fin_rs = at("fin_rs", [P, NB * TT])
        fin_nb = at("fin_nb", [P, NB * TT])
        fin_half = at("fin_half", [P, NB * TT])
        assert top[0] <= w1_offset + E * w1_bytes
        xn_last = nc.alloc_sbuf_tensor_at("xn_last", [P, TT, D], F32, offset=ab_offset)
        bank = [ctx.enter_context(nc.psum_tensor(f"bank{k}", [P, L], F32)) for k in range(8)]
        da, dxp, yp, work = bank[0:2], bank[2:4], bank[4], bank[5:8]
        gate_p, up_p = [bank[0], bank[2]], [bank[1], bank[3]]
        xt_p, at_p, out_p = bank[4], bank[5], bank[6:8]

        packed = sem("packed")
        x_in = sem("x_in")
        sel_in = sem("sel_in")
        wdt_in = sem("wdt_in")
        shared_in = sem("shared_in")
        down_in = sem("down_in")
        tok_in = sem("tok_in")
        const_ready = sem("const_ready")
        dconst = sem("dconst")
        full = [sem(f"work_full{k}") for k in range(3)]
        drained = [sem(f"work_drained{k}") for k in range(3)]
        z_exp = sem("z_exp")
        z_log = sem("z_log")
        delta_ready = sem("delta_ready")
        dx_ready = sem("dx_ready")
        hi_ready = sem("hi_ready")
        lo_ready = sem("lo_ready")
        moved = sem("moved")
        first = {n: sem(f"first_{n}") for n in ("exp", "log", "delta", "dx", "hi", "lo", "moved")}
        decay_in = sem("decay_in")
        drive_in = sem("drive_in")
        decay_ready = sem("decay_ready")
        bx_ready = sem("bx_ready")
        scanned = sem("scanned")
        hc_ready = sem("hc_ready")
        y_quads = sem("y_quads")
        y_taken = sem("y_taken")
        stats = sem("stats")
        bn_step = sem("bn_step")
        rs_step = sem("rs_step")
        rstd_ready = sem("rstd_ready")
        xn_out = sem("xn_out")
        xhi_ready = sem("xhi_ready")
        picked = sem("picked")
        ex_ready = sem("ex_ready")
        rt_step = sem("rt_step")
        ent_ready = sem("ent_ready")
        scattered = sem("scattered")
        gated_ready = [sem("gated_even_ready"), sem("gated_odd_ready")]
        sums_out = sem("sums_out")
        info_ready = sem("info_ready")
        raw_in = [sem(f"raw_in{k}") for k in range(3)]
        hi_split = sem("hi_split")
        lo_split = sem("lo_split")
        w2_in = sem("w2_in")
        row_list_in = [sem(f"row_list_in{k}") for k in range(4)]
        list_in = [sem(f"list_in{k}") for k in range(4)]
        rows_in = [sem(f"rows_in{k}") for k in range(4)]
        xt_full = sem("xt_full")
        xb_hi_ready = sem("xb_hi_ready")
        xbT_ready = sem("xbT_ready")
        gate_full = sem("gate_full")
        up_full = sem("up_full")
        sg_ready = sem("sg_ready")
        ab_ready = sem("ab_ready")
        at_full = sem("at_full")
        aT_ready = sem("aT_ready")
        out_full = sem("out_full")
        ob_ready = sem("ob_ready")
        added = sem("added")
        fin_in = [sem(f"fin_in{k}") for k in range(NB)]
        fin_rstd = sem("fin_rstd")
        padded = sem("padded")
        passed = sem("passed")
        info_step = sem("info_step")
        fin_ready = sem("fin_ready")
        last_ready = sem("last_ready")
        fin_out = sem("fin_out")
        block = ctx.enter_context(nc.Block())

        hl_flat = [t[:, :, :, :].rearrange("p a c l -> p (a c l)") for t in hl]
        bc_flat = bc[:, :, :, :].rearrange("p a s l -> p (a s l)")

        def geometry(n):
            dt, s = divmod(n, NG // DT)
            q, k = s % 4, s // 4
            return dt, q, k, 2 * dt + q // 2, (q % 2) * 4 + k

        def xn_of(m):
            return xn_last if isinstance(m, int) and m == NB - 1 else xn4

        def parity(eng, m):
            return m % 2 if isinstance(m, int) else eng.snap(m % 2)

        def filled(eng, m, name):
            eng.wait_ge(full[BANK[name]], uses(m, name))
            return work[BANK[name]]

        def drain_of(eng, m, name):
            eng.wait_ge(drained[BANK[name]], uses(m, name))

        def alone(eng):
            eng.sem_inc(passed, 1)

        def blocks(eng, step):
            rounds = (NBLK - 5) // 4 - 1
            for c in range(4):
                step(0, c)
            with eng.Fori(0, rounds) as i:
                for c in range(4, 8):
                    step(i, c)
            for c in range(4 * rounds + 4, NBLK):
                step(0, c)

        def start(eng, m):
            return m * L if isinstance(m, int) else eng.snap(m * L)

        @block.tensor
        def _(pe):
            def fill(m, name):
                u = uses(m, name)
                if not (isinstance(u, int) and u == 1):
                    pe.wait_ge(drained[BANK[name]], u - 1)
                return work[BANK[name]]

            def prep(m, name):
                w = None
                tok0 = start(pe, m)
                if name == "dp":
                    if isinstance(m, int):
                        pe.wait_ge(x_in, 16 * (m + 1))
                    w = fill(m, name)
                    for k in range(DT):
                        mm = nc.tensor.matmul(w[0:XR, :], col("wp")[:, k * XR:(k + 1) * XR], xT[:, k, ds(tok0, L)],
                                              start=(k == 0), stop=(k == DT - 1))
                elif name in ("z0", "z1"):
                    w = fill(m, name)
                    dt = int(name[1])
                    if dt == 0:
                        drain_of(pe, m, "dp")
                    mm = nc.tensor.matmul(w[:, :], wdt[:, dt * P:(dt + 1) * P], dps[0:R, :], start=True, stop=True)
                else:
                    w = fill(m, name)
                    if not isinstance(m, int):
                        alone(pe)
                    o = "BC".index(name) * P
                    mm = nc.tensor.matmul(w[:, :], col("bcsel")[R:XR, o:o + P], dps[R:XR, :], start=True, stop=True)
                mm.then_inc(full[BANK[name]], 1)

            def expand(b, n, par, what):
                dt, q, k, c, j = geometry(n)
                ring, done, read = ((da, decay_in, scanned), (dxp, drive_in, bx_ready))[what]
                if not (isinstance(b, int) and NG * b + n < 2):
                    pe.wait_ge(read, NG * b + n - 1)
                nc.tensor.matmul(ring[n % 2][:, :], sel[:, j, :], hl_flat[what][:, ds(par * 4 * L + c * L, L)],
                                 start=True, stop=True).then_inc(done, 1)

            def sum_quad(b, k):
                pe.wait_ge(hc_ready, NG * b + 4 * k + 4)
                if k % 4 == 0 and not (isinstance(b, int) and b == 0 and k == 0):
                    pe.wait_ge(y_taken, DT * b + k // 4)
                for q in range(4):
                    mm = nc.tensor.matmul(yp[32 * q:32 * q + 32, :], col("ysel")[:, (k % 4) * 32:(k % 4) * 32 + 32],
                                          hc[:, (4 * k + q) % 8, :], start=(k % 4 == 0), stop=(k % 4 == 3))
                mm.then_inc(y_quads, 1)

            def post(m, name):
                if name in ("turn0", "turn1"):
                    i = int(name[4])
                    if i == 0:
                        pe.wait_ge(y_taken, DT * (m + 1))
                    w = fill(m, name)
                    for t in range(2):
                        for dt in range(DT):
                            mm = nc.tensor.transpose(w[:, t * D + dt * P:t * D + (dt + 1) * P],
                                                     rT[:, dt, (2 * i + t) * P:(2 * i + t + 1) * P], ident)
                    mm.then_inc(full[BANK[name]], 1)
                elif name in ("back0", "back1"):
                    dt = int(name[4])
                    if dt == 0:
                        drain_of(pe, m, "turn1")
                    w = fill(m, name)
                    for t in range(TT):
                        mm = nc.tensor.transpose(w[:, t * P:(t + 1) * P], xn_of(m)[:, t, dt * P:(dt + 1) * P], ident)
                    mm.then_inc(full[BANK[name]], 1)
                elif name == "logits":
                    drain_of(pe, m, "back1")
                    w = fill(m, name)
                    terms = [(x, k) for x in (xhi, xlo) for k in range(DT)]
                    for i, (x, k) in enumerate(terms):
                        mm = nc.tensor.matmul(w[0:2 * E, :], rw[:, k, :, :].rearrange("p s e -> p (s e)"), x[:, k, :],
                                              start=(i == 0), stop=(i == len(terms) - 1))
                    mm.then_inc(full[BANK[name]], 1)
                elif name == "tokens":
                    drain_of(pe, m, "logits")
                    w = fill(m, name)
                    alone(pe)
                    for t in range(TT):
                        mm = nc.tensor.transpose(w[:, t * 2 * E:(t + 1) * 2 * E], lgt[:, t * P:(t + 1) * P],
                                                 ident[0:2 * E, 0:2 * E])
                    mm.then_inc(full[BANK[name]], 1)
                elif name == "ranks":
                    pe.wait_ge(picked, m + 1)
                    w = fill(m, name)
                    nc.tensor.matmul(w[:, 0:TT * E], lower[:, 0, :], oh_b[:, :, :].rearrange("p t e -> p (t e)"),
                                     start=True, stop=True)
                    nc.tensor.matmul(w[:, TT * E:2 * TT * E], lower[:, 1, :],
                                     oh_b[:, :, :].rearrange("p t e -> p (t e)"),
                                     start=True, stop=True).then_inc(full[BANK[name]], 1)
                elif name[0] in "gu":
                    i, side = int(name[1:]), "gu".index(name[0])
                    w = fill(m, name)
                    terms = [(a, x, k) for a, x in ((wg_hi, xhi), (wg_hi, xlo), (wg_lo, xhi)) for k in range(DT)]
                    for t, (a, x, k) in enumerate(terms):
                        mm = nc.tensor.matmul(w[:, :], a[:, side, k, i * P:(i + 1) * P], x[:, k, :],
                                              start=(t == 0), stop=(t == len(terms) - 1))
                    mm.then_inc(full[BANK[name]], 1)
                else:
                    i, piece = int(name[4]), int(name[6])
                    w = work[BANK[name[:5]]] if piece else fill(m, name[:5])
                    t = piece // 2
                    for k in range(piece % 2 * NI // 2, (piece % 2 + 1) * NI // 2):
                        if i == 0 and t == 0:
                            pe.wait_ge(gated_ready[k % 2], NI // 2 * m + k // 2 + 1)
                        mm = nc.tensor.matmul(w[:, t * D:(t + 1) * D],
                                              act[:, k, (2 * i + t) * P:(2 * i + t + 1) * P], wd[:, k, :],
                                              start=(k == 0), stop=(k == NI - 1))
                    if piece == 3:
                        mm.then_inc(full[BANK[name[:5]]], 1)

            def batch(b, groups):
                par = parity(pe, b)
                for n in groups:
                    ahead = isinstance(b, int) and b == 0
                    if n == 0 and ahead:
                        pe.wait_ge(first["moved"], 128)
                    if n == (NG // DT - 1 if ahead else 0):
                        pe.wait_ge(moved, 128 * (b + 1))
                    if n == 0:
                        expand(b, 0, par, 1)
                    expand(b, n, par, 0)
                    if n + 1 < NG:
                        expand(b, n + 1, par, 1)
                    if n % 4 == 3 and n > 3:
                        sum_quad(b, n // 4 - 1)
                    if n == LAST_QUAD_AT and not (isinstance(b, int) and b == 0):
                        sum_quad(b - 1, NQ - 1)
                    for m, name in side_steps(TENSOR_AT, b, n):
                        (prep if name in PREP else post)(m, name)

            pe.wait_ge(packed, 16)
            pe.wait_ge(wdt_in, 16)
            for name in ("dp", "z0", "z1", "B", "C"):
                prep(0, name)
            pe.wait_ge(const_ready, SCAN_ACT)
            batch(0, FIRST)
            batch(0, SECOND)
            batch(1, FIRST)
            pe.wait_ge(const_ready, SETUP_ACT)
            pe.wait_ge(dconst, SETUP_DVE)
            pe.wait_ge(down_in, 16)
            with pe.Fori(1, NB - 1) as b:
                batch(b, SECOND)
                batch(b + 1, FIRST)
            batch(NB - 1, SECOND)
            for piece in range(4):
                post(NB - 2, f"down0.{piece}")
                if piece == 0:
                    sum_quad(NB - 1, NQ - 1)
            for name in TURN:
                post(NB - 1, name)
            for piece in range(4):
                post(NB - 2, f"down1.{piece}")
            for n, name in last_post(TENSOR_AT):
                post(NB - 1, name)
            for name in DOWN:
                for piece in range(4):
                    post(NB - 1, f"{name}.{piece}")

            w1_flat = w1[:, :, :, :, :].rearrange("p e s k n -> p (e s k n)")
            w2_flat = w2[:, :, :, :].rearrange("p e k n -> p (e k n)")

            def turn_rows(i, c):
                pe.wait_ge(rows_in[c % 4], 16 * i + 16 * (c // 4 + 1))
                if c >= 1:
                    pe.wait_ge(xbT_ready, 4 * i + c)
                for dt in range(DT):
                    mm = nc.tensor.transpose(xt_p[:, dt * P:(dt + 1) * P], xb[:, c % 4, dt * P:(dt + 1) * P], ident)
                mm.then_inc(xt_full, 1)

            def up(i, c):
                expert = pe.value_load(info[0:1, 0, ds(i * 4 + c, 1)], min_val=0, max_val=E - 1)
                base = pe.snap((E - 1) * (2 * DT * 2 * INTER) - expert * (2 * DT * 2 * INTER))
                pe.wait_ge(lo_split, pe.snap(expert * DT + DT))
                alone(pe)
                pe.wait_ge(xbT_ready, 4 * i + c + 1)
                if c >= 2:
                    pe.wait_ge(ab_ready, 4 * i + c - 1)
                for half, (dst, done) in enumerate(((gate_p, gate_full), (up_p, up_full))):
                    terms = [(k, x, w) for k in range(DT) for x, w in ((0, 0), (0, 1), (1, 0))]
                    for t, (k, x, w) in enumerate(terms):
                        mm = nc.tensor.matmul(dst[c % 2][:, :], xbT[:, c % 2, x, k, :],
                                              w1_flat[:, ds(base + ((w * DT + k) * 2 + half) * INTER, INTER)],
                                              start=(t == 0), stop=(t == len(terms) - 1))
                    mm.then_inc(done, 1)

            def turn_act(i, c):
                pe.wait_ge(ab_ready, 4 * i + c + 1)
                if c >= 1:
                    pe.wait_ge(aT_ready, 4 * i + c)
                for k in range(INTER // P):
                    mm = nc.tensor.transpose(at_p[:, k * P:(k + 1) * P], ab[:, c % 2, k * P:(k + 1) * P], ident)
                mm.then_inc(at_full, 1)

            def down(i, c):
                expert = pe.value_load(info[0:1, 0, ds(i * 4 + c, 1)], min_val=0, max_val=E - 1)
                base = pe.snap(expert * (INTER // P * D))
                pe.wait_ge(aT_ready, 4 * i + c + 1)
                if c >= 2:
                    pe.wait_ge(ob_ready, 4 * i + c - 1)
                for k in range(INTER // P):
                    mm = nc.tensor.matmul(out_p[c % 2][:, 0:D], aT[:, c % 2, k * P:(k + 1) * P],
                                          w2_flat[:, ds(base + k * D, D)], start=(k == 0), stop=(k == INTER // P - 1))
                mm.then_inc(out_full, 1)

            pe.wait_ge(info_ready, 1)
            turn_rows(0, 0)
            turn_rows(0, 1)
            pe.wait_ge(w2_in, 16)
            up(0, 0)

            def step(i, c):
                if c + 2 < NBLK:
                    turn_rows(i, c + 2)
                if c + 1 < NBLK:
                    up(i, c + 1)
                if c >= 1:
                    down(i, c - 1)
                turn_act(i, c)

            blocks(pe, step)
            down(0, NBLK - 1)

        @block.scalar
        def _(se):
            act_ = nc.scalar.activation

            def prep(m, name):
                if name == "dp":
                    w = filled(se, m, name)
                    act_(dps[:, :], w[0:XR, :], ACT.Copy).then_inc(drained[BANK[name]], 1)
                elif name in ("z0", "z1"):
                    dt = int(name[1])
                    if not (isinstance(m, int) and m == 0):
                        se.wait_ge(lo_ready, DT * m)
                    w = filled(se, m, name)
                    bias = col("bdt")[:, dt:dt + 1]
                    act_(lnt[:, dt, :], w[:, :], ACT.Abs, bias=bias)
                    act_(rel[:, dt, :], w[:, :], ACT.Relu, bias=bias).then_inc(drained[BANK[name]], 1)
                elif name == "log":
                    drain_of(se, m, "z1")
                    act_(lnt[:, :, :], lnt[:, :, :], ACT.Exp, scale=-1.0).then_inc(z_exp, 1)
                    se.wait_ge(z_exp, m + 1)
                    act_(lnt[:, :, :], lnt[:, :, :], ACT.Ln, bias=1.0).then_inc(z_log, 1)
                elif name in ("B", "C"):
                    w = filled(se, m, name)
                    if not (isinstance(m, int) and m < 2):
                        se.wait_ge(hc_ready, NG * (m - 1))
                    o = parity(se, m) * 2 * L + "BC".index(name) * L
                    act_(bc_flat[:, ds(o, L)], w[:, :], ACT.Copy).then_inc(drained[BANK[name]], 1)
                else:
                    i = int(name[2])
                    se.wait_ge((delta_ready, dx_ready)[i], m + 1)
                    if not (isinstance(m, int) and m == 0):
                        se.wait_ge(moved, 128 * m)
                    act_(hi[i][:, :, :], (rel, lnt)[i][:, :, :], ACT.Copy).then_inc(hi_ready, 1)

            def post(m, name):
                if name in ("turn0", "turn1"):
                    i = int(name[4])
                    se.wait_ge(rstd_ready, 2 * m + i + 1)
                    if xn_of(m) is xn4:
                        if i == 0:
                            se.wait_ge(xn_out, 16 * (m + 1))
                        if not (isinstance(m, int) and m == 0):
                            drain_of(se, m - 1, f"down{i}")
                    w = filled(se, m, name)
                    for t in range(2):
                        a = act_(xn_of(m)[:, 2 * i + t, :], w[:, t * D:(t + 1) * D], ACT.Identity,
                                 bias=nbias[:, 2 * i + t:2 * i + t + 1], scale=rstd[:, 2 * i + t:2 * i + t + 1])
                    a.then_inc(drained[BANK[name]], 1)
                elif name in ("back0", "back1"):
                    dt = int(name[4])
                    w = filled(se, m, name)
                    act_(xhi[:, dt, :], w[:, :], ACT.Copy).then_inc(xhi_ready, 1)
                elif name == "logits":
                    w = filled(se, m, name)
                    act_(lgt[:, :], w[0:2 * E, :], ACT.Copy).then_inc(drained[BANK[name]], 1)
                elif name == "ex":
                    se.wait_ge(picked, m + 1)
                    act_(ex[:, :], gap[:, :], ACT.Exp).then_inc(ex_ready, 1)
                else:
                    i = int(name[1:])
                    w = filled(se, m, name)
                    if i == 0:
                        se.wait_ge(sums_out, 16 * (m + 1))
                    if i >= 2:
                        se.wait_ge(gated_ready[i % 2], NI // 2 * m + i // 2)
                    act_(gh[:, i % 2, :], w[:, :], ACT.Copy, scale=0.5)
                    act_(th[:, i % 2, :], w[:, :], ACT.Tanh, scale=0.5).then_inc(drained[BANK[name]], 1)

            def batch(b, groups):
                for n in groups:
                    se.wait_ge(decay_in, NG * b + n + 1)
                    act_(da[n % 2][:, :], da[n % 2][:, :], ACT.Exp,
                         scale=aneg[:, n:n + 1]).then_inc(decay_ready, 1)
                    for m, name in side_steps(SCALAR_AT, b, n):
                        (prep if name in PREP_STEPS else post)(m, name)
                    if isinstance(b, int) and b == 0 and n in SHARED_ACT:
                        side, k = divmod(SHARED_ACT[n], DT)
                        se.wait_ge(shared_in, 16)
                        act_(wg_hi[:, side, k, :], wg_raw[:, side, k, :], ACT.Copy).then_inc(const_ready, 1)

            se.wait_ge(packed, 16)
            act_(aneg[:, :], col("alog"), ACT.Exp).then_inc(const_ready, 1)
            act_(rw[:, :, 0, :], col("rw").rearrange("p (k e) -> p k e", e=E), ACT.Copy).then_inc(const_ready, 1)
            act_(lower[:, :, :].rearrange("p k e -> p (k e)"), col("lower"), ACT.Copy).then_inc(const_ready, 1)
            se.wait_ge(sel_in, 16)
            act_(sel[:, :, :], sel_raw[:, :, :], ACT.Copy).then_inc(const_ready, 1)
            for name in ("dp", "z0", "z1"):
                prep(0, name)
            drain_of(se, 0, "z1")
            for dt in range(DT):
                act_(lnt[:, dt, :], lnt[:, dt, :], ACT.Exp, scale=-1.0).then_inc((first["exp"], z_exp)[dt], 1)
            for dt in range(DT):
                se.wait_ge((first["exp"], z_exp)[dt], 1)
                act_(lnt[:, dt, :], lnt[:, dt, :], ACT.Ln, bias=1.0).then_inc((first["log"], z_log)[dt], 1)
            for dt in range(DT):
                for i in range(2):
                    se.wait_ge(((first["delta"], first["dx"]), (delta_ready, dx_ready))[dt][i], 1)
                    act_(hi[i][:, dt, :], (rel, lnt)[i][:, dt, :],
                         ACT.Copy).then_inc((first["hi"], hi_ready)[dt], 1)
                prep(0, "BC"[dt])
            se.wait_ge(dconst, SCAN_DVE)
            batch(0, FIRST)
            batch(0, SECOND)
            batch(1, FIRST)
            with se.Fori(1, NB - 1) as b:
                batch(b, SECOND)
                batch(b + 1, FIRST)
            batch(NB - 1, SECOND)

            def split(j):
                se.wait_ge(raw_in[j % 3], 16 * (j // 3 + 1))
                if j in W1_FREE:
                    filled(se, NB - 1, W1_FREE[j])
                act_(w1[:, E - 1 - j // DT, 0, j % DT, :], w1_raw[:, j % 3, :], ACT.Copy).then_inc(hi_split, 1)

            for name in TURN:
                post(NB - 1, name)
            for j in range(4):
                split(j)
            for n, name in last_post(SCALAR_AT):
                post(NB - 1, name)
                for j in SPLIT_AT.get(name, ()):
                    split(j)
            for j in range(W1_EARLY, 12):
                split(j)

            def rows(i, c):
                se.wait_ge(xt_full, 4 * i + c + 1)
                if c >= 2:
                    se.wait_ge(up_full, 4 * i + c - 1)
                act_(xbT[:, c % 2, 0, :, :].rearrange("p k t -> p (k t)"), xt_p[:, 0:D],
                     ACT.Copy).then_inc(xb_hi_ready, 1)

            def silu(i, c):
                se.wait_ge(gate_full, 4 * i + c + 1)
                if c >= 2:
                    se.wait_ge(ab_ready, 4 * i + c - 1)
                act_(sg[:, c % 2, :], gate_p[c % 2][:, :], ACT.Silu).then_inc(sg_ready, 1)

            def scale(i, c):
                se.wait_ge(out_full, 4 * i + c + 1)
                se.wait_ge(list_in[c % 4], 16 * i + 16 * (c // 4 + 1))
                if c >= 2:
                    se.wait_ge(added, 16 * (4 * i + c - 1))
                act_(ob[:, c % 2, :], out_p[c % 2][:, 0:D], ACT.Copy,
                     scale=lst[:, c % 4, 1:2].bitcast(F32)).then_inc(ob_ready, 1)

            rows(0, 0)
            rows(0, 1)
            for j in range(12, DT * E):
                split(j)
            silu(0, 0)

            def step(i, c):
                if c + 2 < NBLK:
                    rows(i, c + 2)
                if c + 1 < NBLK:
                    silu(i, c + 1)
                if c >= 1:
                    scale(i, c - 1)

            blocks(se, step)
            scale(0, NBLK - 1)
            for b in range(NB - 1):
                se.wait_ge(fin_rstd, b + 1)
                for t in range(TT):
                    j = b * TT + t
                    a = act_(fin_o[:, b, t, :], fin[:, b, t, :], ACT.Identity,
                             bias=fin_nb[:, j:j + 1], scale=fin_rs[:, j:j + 1])
                a.then_inc(fin_ready, 1)

        @block.vector
        def _(ve_):
            tt = nc.vector.tensor_tensor
            chain = {"k": 0}

            def prep(m, name):
                if name == "delta":
                    ve_.wait_ge(z_log, m + 1)
                    tt(out=rel[:, :, :], in0=rel[:, :, :], in1=lnt[:, :, :], op=ALU.add).then_inc(delta_ready, 1)
                elif name == "dx":
                    t0 = start(ve_, m)
                    ve_.wait_ge(delta_ready, m + 1)
                    if isinstance(m, int):
                        ve_.wait_ge(x_in, 16 * (m + 1))
                    tt(out=lnt[:, :, :], in0=rel[:, :, :], in1=xT[:, :, ds(t0, L)], op=ALU.mult).then_inc(dx_ready, 1)

            def drive(b, n, bo):
                ve_.wait_ge(drive_in, NG * b + n + 1)
                if n == 0:
                    drain_of(ve_, b, "B")
                if not (isinstance(b, int) and NG * b + n < 2):
                    ve_.wait_ge(scanned, NG * b + n - 1)
                tt(out=bx[:, n % 2, :], in0=dxp[n % 2][:, :], in1=bc_flat[:, ds(bo, L)],
                   op=ALU.mult).then_inc(bx_ready, 1)

            def scan(b, n):
                ve_.wait_ge(decay_ready, NG * b + n + 1)
                ve_.wait_ge(bx_ready, NG * b + n + 1)
                if not (isinstance(b, int) and NG * b + n < 4):
                    ve_.wait_ge(hc_ready, NG * b + n - 3)
                nc.vector.tensor_tensor_scan(out=h[:, n % 4, :], data0=da[n % 2][:, :], data1=bx[:, n % 2, :],
                                             initial=0.0, op0=ALU.mult, op1=ALU.add).then_inc(scanned, 1)

            def take_y(b, dt):
                t0 = start(ve_, b)
                ve_.wait_ge(y_quads, NQ * b + 4 * dt + 4)
                nc.vector.scalar_tensor_tensor(out=rT[:, dt, :], in0=xT[:, dt, ds(t0, L)], scalar=dp1[:, dt:dt + 1],
                                               in1=yp[:, :], op0=ALU.mult, op1=ALU.add).then_inc(y_taken, 1)

            def post(m, name):
                def link(instr):
                    chain["k"] += 1
                    instr.then_inc(rt_step, 1)
                    ve_.wait_ge(rt_step, RT_STEPS * m + chain["k"])

                def per_token(ap):
                    return ap.unsqueeze(2).to_broadcast([P, TT, E])

                def per_expert(ap):
                    return ap.unsqueeze(1).to_broadcast([P, TT, E])

                if name in ("turn0", "turn1"):
                    i = int(name[4])
                    w = filled(ve_, m, name)
                    for t in range(2):
                        s = nc.vector.bn_stats(bn[:, 2 * i + t, :], w[:, t * D:(t + 1) * D])
                    s.then_inc(bn_step, 1)
                    ve_.wait_ge(bn_step, 2 * m + i + 1)
                    alone(ve_)
                    for t in range(2):
                        s = nc.vector.bn_aggr(mv[:, 2 * i + t, :], bn[:, 2 * i + t, :])
                    s.then_inc(stats, 1)
                elif name in ("back0", "back1"):
                    dt = int(name[4])
                    ve_.wait_ge(xhi_ready, DT * m + dt + 1)
                    w = filled(ve_, m, name)
                    tt(out=xlo[:, dt, :], in0=w[:, :], in1=xhi[:, dt, :].bitcast(F32),
                       op=ALU.subtract).then_inc(drained[BANK[name]], 1)
                elif name == "tokens":
                    chain["k"] = 0
                    w = filled(ve_, m, name)
                    parts = w[:, 0:2 * TT * E].rearrange("p (t s e) -> p t s e", s=2, e=E)
                    link(nc.vector.tensor_copy(lg[:, :, :], parts[:, :, 0, :]))
                    tt(out=lg[:, :, :], in0=lg[:, :, :], in1=parts[:, :, 1, :],
                       op=ALU.add).then_inc(drained[BANK[name]], 1)
                elif name in ("first", "second"):
                    k = 1 if name == "second" else 0
                    src = (lg, lg2)[k]
                    if k == 0:
                        drain_of(ve_, m, "tokens")
                    link(nc.vector.tensor_reduce(out=mx[:, k, :], in_=src[:, :, :], axis=AX, op=ALU.max))
                    link(tt(out=eq[:, k], in0=src[:, :, :], in1=per_token(mx[:, k, :]), op=ALU.is_equal))
                    link(tt(out=key[:, k], in0=eq[:, k], in1=per_expert(rev), op=ALU.mult))
                    link(nc.vector.tensor_reduce(out=kk[:, k, :], in_=key[:, k], axis=AX, op=ALU.max))
                    link(tt(out=oh[:, k], in0=per_expert(rev), in1=per_token(kk[:, k, :]), op=ALU.is_equal))
                    if k == 0:
                        link(nc.vector.scalar_tensor_tensor(
                            out=lg2[:, :, :], in0=oh[:, 0], scalar=-3e38, in1=lg[:, :, :],
                            op0=ALU.mult, op1=ALU.add))
                    else:
                        link(tt(out=gap[:, :], in0=mx[:, 1, :], in1=mx[:, 0, :], op=ALU.subtract))
                        tt(out=oh_b[:, :, :], in0=oh[:, 0], in1=oh[:, 1], op=ALU.add).then_inc(picked, 1)
                elif name == "ex":
                    ve_.wait_ge(ex_ready, m + 1)
                    link(nc.vector.tensor_scalar_add(den[:, :], ex[:, :], 1.0))
                    link(nc.vector.reciprocal(sc[:, 0, :], den[:, :]))
                    link(tt(out=sc[:, 1, :], in0=ex[:, :], in1=sc[:, 0, :], op=ALU.mult))
                elif name == "ranks":
                    w = filled(ve_, m, name)
                    tot = w[:, TT * E:2 * TT * E].rearrange("p (t e) -> p t e", e=E)
                    for t in range(TT):
                        link(tt(out=offs[:, t + 1, :], in0=offs[:, t, :], in1=tot[:, t, :], op=ALU.add))
                    tt(out=rk[:, :, :], in0=w[:, 0:TT * E].rearrange("p (t e) -> p t e", e=E),
                       in1=offs[:, 0:TT, :], op=ALU.add).then_inc(drained[BANK[name]], 1)
                    drain_of(ve_, m, name)
                    link(nc.vector.tensor_copy(offs[:, 0, :], offs[:, TT, :]))
                    link(tt(out=rk2[:, :, :], in0=rk[:, :, :], in1=per_expert(region), op=ALU.add))
                elif name in ("rows0", "rows1"):
                    k = int(name[4])
                    t0 = m * TT if isinstance(m, int) else ve_.snap(m * TT)
                    link(tt(out=pr[:, k], in0=oh[:, k], in1=rk2[:, :, :], op=ALU.mult))
                    link(nc.vector.tensor_reduce(out=posf[:, k, :], in_=pr[:, k], axis=AX, op=ALU.add))
                    link(nc.vector.tensor_copy(ent[:, k, :, 1:2].bitcast(F32), sc[:, k, :].unsqueeze(2)))
                    alone(ve_)
                    link(nc.vector.tensor_copy(ent[:, k, :, 0:1], tok[:, ds(t0, TT)].unsqueeze(2)))
                    if k == 1:
                        assert chain["k"] == RT_STEPS, chain
                        nc.vector.tensor_copy(pos[:, :, :], posf[:, :, :]).then_inc(ent_ready, 1)
                elif name[0] == "u":
                    i = int(name[1:])
                    drain_of(ve_, m, f"g{i}")
                    w = filled(ve_, m, name)
                    nc.vector.scalar_tensor_tensor(out=act[:, i, :], in0=th[:, i % 2, :], scalar=1.0, in1=w[:, :],
                                                   op0=ALU.add, op1=ALU.mult).then_inc(drained[BANK[name]], 1)
                    if i % 2 and not (isinstance(m, int) and m == NB - 1 and i < NI - 1):
                        drain_of(ve_, m, name)
                        tt(out=act[:, i, :], in0=act[:, i, :], in1=gh[:, i % 2, :],
                           op=ALU.mult).then_inc(gated_ready[1], 1)
                else:
                    i = int(name[4])
                    last = isinstance(m, int) and m == NB - 1
                    if last:
                        ve_.wait_ge(xn_out, 16 * (m + 2))
                    w = filled(ve_, m, name)
                    x4 = xn_of(m)[:, 2 * i:2 * i + 2, :].rearrange("p t d -> p (t d)")
                    tt(out=x4 if last else gh[:, i, :], in0=w[:, :], in1=x4,
                       op=ALU.add).then_inc(drained[BANK[name]], 1)

            def batch(b, groups):
                bo = parity(ve_, b) * 2 * L
                if not isinstance(bo, int):
                    bo = ve_.snap(bo)
                for n in groups:
                    if n == 0:
                        drive(b, 0, bo)
                    if n + 1 < NG:
                        drive(b, n + 1, bo)
                    scan(b, n)
                    if n == Y1_AT and not (isinstance(b, int) and b == 0):
                        take_y(b - 1, 1)
                    if n == Y0_AT:
                        take_y(b, 0)
                    for m, name in side_steps(VECTOR_AT, b, n):
                        (prep if name in PREP_STEPS else post)(m, name)
                    if isinstance(b, int) and b == 0 and n in SHARED_DVE:
                        side, k = divmod(SHARED_DVE[n], DT)
                        ve_.wait_ge(const_ready, SCAN_ACT + SHARED_DVE[n] + 1)
                        tt(out=wg_lo[:, side, k, :], in0=wg_raw[:, side, k, :],
                           in1=wg_hi[:, side, k, :].bitcast(F32), op=ALU.subtract).then_inc(dconst, 1)

            nc.vector.memset(mhalf[:, :], -0.5).then_inc(dconst, 1)
            nc.vector.memset(offs[:, 0, :], 0.0).then_inc(dconst, 1)
            nc.vector.memset(xn4[:, 0, :], 0.0).then_inc(dconst, 1)
            ve_.wait_ge(packed, 16)
            nc.vector.tensor_scalar_add(dp1[:, :], col("dpar"), 1.0).then_inc(dconst, 1)
            ve_.wait_ge(const_ready, 2)
            nc.vector.tensor_scalar_mul(aneg[:, :], aneg[:, :], -1.0).then_inc(dconst, 1)
            tt(out=rw[:, :, 1, :], in0=col("rw").rearrange("p (k e) -> p k e", e=E),
               in1=rw[:, :, 0, :].bitcast(F32), op=ALU.subtract).then_inc(dconst, 1)
            ve_.wait_ge(x_in, 16)
            for dt in range(DT):
                ve_.wait_ge((first["log"], z_log)[dt], 1)
                tt(out=rel[:, dt, :], in0=rel[:, dt, :], in1=lnt[:, dt, :],
                   op=ALU.add).then_inc((first["delta"], delta_ready)[dt], 1)
                ve_.wait_ge((first["delta"], delta_ready)[dt], 1)
                tt(out=lnt[:, dt, :], in0=rel[:, dt, :], in1=xT[:, dt, 0:L],
                   op=ALU.mult).then_inc((first["dx"], dx_ready)[dt], 1)
                for i in range(2):
                    ve_.wait_ge((first["hi"], hi_ready)[dt], i + 1)
                    if i:
                        ve_.wait_ge((first["dx"], dx_ready)[dt], 1)
                    tt(out=lo[i][:, dt, :], in0=(rel, lnt)[i][:, dt, :], in1=hi[i][:, dt, :].bitcast(F32),
                       op=ALU.subtract).then_inc((first["lo"], lo_ready)[dt], 1)
            ve_.wait_ge(dconst, SCAN_DVE)
            batch(0, FIRST)
            batch(0, SECOND)
            batch(1, FIRST)
            ve_.wait_ge(dconst, SETUP_DVE)
            with ve_.Fori(1, NB - 1) as b:
                batch(b, SECOND)
                batch(b + 1, FIRST)
            batch(NB - 1, SECOND)
            take_y(NB - 1, 1)
            post(NB - 2, "down0")
            for name in TURN:
                post(NB - 1, name)

            def split(j):
                ve_.wait_ge(hi_split, j + 1)
                at_ = w1[:, E - 1 - j // DT, :, j % DT, :]
                tt(out=at_[:, 1, :], in0=w1_raw[:, j % 3, :], in1=at_[:, 0, :].bitcast(F32),
                   op=ALU.subtract).then_inc(lo_split, 1)

            for j in range(3):
                split(j)
            post(NB - 2, "down1")
            split(3)
            for n, name in last_post(VECTOR_AT):
                post(NB - 1, name)
                for j in SPLIT_AFTER.get(name, ()):
                    split(j)

            blk = {"k": 0}

            def link(instr):
                blk["k"] += 1
                instr.then_inc(info_step, 1)
                ve_.wait_ge(info_step, blk["k"])

            def by_expert(ap):
                return ap.unsqueeze(1).to_broadcast([1, NBLK, E])

            def by_block(ap):
                return ap.unsqueeze(2).to_broadcast([1, NBLK, E])

            number, expert = col("block", 1), col("expert", 1)
            link(nc.vector.tensor_scalar_add(cnti[:, 0, :], offs[0:1, 0, :], float(P - 1)))
            link(nc.vector.tensor_single_scalar(cnti[:, 1, :], cnti[:, 0, :], 7, op=ALU.arith_shift_right))
            link(nc.vector.tensor_copy(cnt[:, 0, :], cnti[:, 1, :]))
            link(nc.vector.memset(cnt[:, 1, :], 1.0))
            link(nc.vector.tensor_tensor_scan(out=cnt[:, 2, :], data0=cnt[:, 1, :], data1=cnt[:, 0, :],
                                              initial=0.0, op0=ALU.mult, op1=ALU.add))
            link(tt(out=cnt[:, 3, :], in0=cnt[:, 2, :], in1=cnt[:, 0, :], op=ALU.subtract))
            link(tt(out=btw[:, :, :], in0=by_block(number), in1=by_expert(cnt[:, 2, :]), op=ALU.is_ge))
            link(nc.vector.tensor_reduce(out=btc[:, 0, :], in_=btw[:, :, :], axis=AX, op=ALU.add))
            link(nc.vector.tensor_scalar(out=btc[:, 1, :], in0=btc[:, 0, :], scalar1=float(E), scalar2=None,
                                         op0=ALU.is_lt))
            link(nc.vector.tensor_scalar(out=btc[:, 2, :], in0=btc[:, 0, :], scalar1=float(E - 1), scalar2=None,
                                         op0=ALU.min))
            link(tt(out=btw[:, :, :], in0=by_expert(expert), in1=by_block(btc[:, 2, :]), op=ALU.is_equal))
            link(tt(out=btw[:, :, :], in0=btw[:, :, :], in1=by_expert(cnt[:, 3, :]), op=ALU.mult))
            link(nc.vector.tensor_reduce(out=btc[:, 3, :], in_=btw[:, :, :], axis=AX, op=ALU.add))
            link(tt(out=btc[:, 4, :], in0=number, in1=btc[:, 3, :], op=ALU.subtract))
            link(nc.vector.tensor_scalar(out=btc[:, 5, :], in0=btc[:, 4, :], scalar1=float(P),
                                         scalar2=-float(E * REGION), op0=ALU.mult, op1=ALU.add))
            link(nc.vector.scalar_tensor_tensor(out=btc[:, 6, :], in0=btc[:, 2, :], scalar=float(REGION),
                                                in1=btc[:, 5, :], op0=ALU.mult, op1=ALU.add))
            link(tt(out=btc[:, 7, :], in0=btc[:, 6, :], in1=btc[:, 1, :], op=ALU.mult))
            link(nc.vector.tensor_copy(info[:, 0, :], btc[:, 2, :]))
            nc.vector.tensor_scalar_add(info[:, 1, :], btc[:, 7, :], float(E * REGION)).then_inc(info_ready, 1)
            for j in (8, 9):
                split(j)
            post(NB - 1, "down0")
            for j in (10, 11):
                split(j)
            post(NB - 1, "down1")

            def rows_lo(i, c):
                ve_.wait_ge(xb_hi_ready, 4 * i + c + 1)
                at_ = xbT[:, c % 2, :, :, :].rearrange("p s k t -> p s (k t)")
                tt(out=at_[:, 1, :], in0=xt_p[:, 0:D], in1=at_[:, 0, :].bitcast(F32),
                   op=ALU.subtract).then_inc(xbT_ready, 1)

            def gated(i, c):
                ve_.wait_ge(sg_ready, 4 * i + c + 1)
                ve_.wait_ge(up_full, 4 * i + c + 1)
                if c >= 2:
                    ve_.wait_ge(at_full, 4 * i + c - 1)
                tt(out=ab[:, c % 2, :], in0=up_p[c % 2][:, :], in1=sg[:, c % 2, :], op=ALU.mult).then_inc(ab_ready, 1)

            def turned(i, c):
                ve_.wait_ge(at_full, 4 * i + c + 1)
                if c >= 2:
                    ve_.wait_ge(out_full, 4 * i + c - 1)
                nc.vector.tensor_copy(aT[:, c % 2, :], at_p[:, :]).then_inc(aT_ready, 1)

            rows_lo(0, 0)
            rows_lo(0, 1)
            for j in range(12, DT * E):
                split(j)
            ve_.wait_ge(sums_out, 16 * (NB + 1))
            gated(0, 0)

            def step(i, c):
                if c + 2 < NBLK:
                    rows_lo(i, c + 2)
                if c + 1 < NBLK:
                    gated(i, c + 1)
                turned(i, c)

            blocks(ve_, step)
            for b in range(NB):
                ve_.wait_ge(fin_in[b], 16)
                for t in range(TT):
                    s = nc.vector.bn_stats(fin_bn[:, b * TT + t, :], fin[:, b, t, :])
                s.then_inc(bn_step, 1)
                ve_.wait_ge(bn_step, 2 * NB + b + 1)
                for t in range(TT):
                    s = nc.vector.bn_aggr(fin_mv[:, b * TT + t, :], fin_bn[:, b * TT + t, :])
                s.then_inc(stats, 1)
            ve_.wait_ge(fin_rstd, NB)
            for t in range(TT):
                j = (NB - 1) * TT + t
                s = nc.vector.tensor_scalar(out=fin_o[:, NB - 1, t, :], in0=fin[:, NB - 1, t, :],
                                            scalar1=fin_rs[:, j:j + 1], scalar2=fin_nb[:, j:j + 1],
                                            op0=ALU.mult, op1=ALU.add)
            s.then_inc(last_ready, 1)

        @block.gpsimd
        def _(po):
            def rstd_of(lo_, hi_, done, k, buffers):
                r = slice(lo_, hi_)
                mv, ve, mhalf, rstd, nbias = buffers
                var, mean = mv[:, r, 1:2].squeeze(2), mv[:, r, 0:1].squeeze(2)
                alone(po)
                po.tensor_scalar(out=ve[:, r], in0=var, scalar1=EPS, scalar2=None, op0=ALU.add).then_inc(rs_step, 1)
                own = 1 if mv is fin_mv else 0
                po.wait_ge(rs_step, 2 * k + 1 + own)
                po.tensor_tensor(out=rstd[:, r], in0=ve[:, r], in1=mhalf[:, r], op=ALU.pow)
                po.tensor_scalar(out=nbias[:, r], in0=mean, scalar1=-1.0, scalar2=None,
                                 op0=ALU.mult).then_inc(rs_step, 1)
                po.wait_ge(rs_step, 2 * k + 2 + own)
                alone(po)
                po.tensor_tensor(out=nbias[:, r], in0=nbias[:, r], in1=rstd[:, r], op=ALU.mult).then_inc(done, 1)

            def prep(m, name):
                i = int(name[2])
                po.wait_ge(hi_ready, DT * m + i + 1)
                po.wait_ge(moved, 128 * m)
                alone(po)
                po.tensor_tensor(out=lo[i][:, :, :], in0=(rel, lnt)[i][:, :, :], in1=hi[i][:, :, :].bitcast(F32),
                                 op=ALU.subtract).then_inc(lo_ready, 1)

            def post(m, name):
                if name in ("turn0", "turn1"):
                    i = int(name[4])
                    po.wait_ge(stats, 2 * m + i + 1)
                    rstd_of(2 * i, 2 * i + 2, rstd_ready, 2 * m + i, (mv, ve, mhalf, rstd, nbias))
                elif name[0] == "g":
                    i = int(name[1:])
                    drain_of(po, m, f"u{i}")
                    alone(po)
                    po.tensor_tensor(out=act[:, i, :], in0=act[:, i, :], in1=gh[:, i % 2, :],
                                     op=ALU.mult).then_inc(gated_ready[i % 2], 1)
                elif name == "landed":
                    po.wait_ge(scattered, 128 * (m + 1))
                    alone(po)
                else:
                    k, t = divmod(int(name[7:]), TT)
                    po.wait_ge(ent_ready, m + 1)
                    alone(po)
                    po.indirect_dma_start(out=list_d, in_=ent[:, k, t, :], in_offset=None,
                                          out_offset=bass.IndirectOffsetOnAxis(ap=pos[:, k, t:t + 1], axis=0)
                                          ).then_inc(scattered, 16)

            def batch(b, groups):
                co = parity(po, b) * 2 * L + L
                if not isinstance(co, int):
                    co = po.snap(co)
                for n in groups:
                    po.wait_ge(scanned, NG * b + n + 1)
                    if n == 0:
                        drain_of(po, b, "C")
                    if not (isinstance(b, int) and NG * b + n < 8):
                        po.wait_ge(y_quads, NQ * b + (n - 8) // 4 + 1)
                    alone(po)
                    po.tensor_tensor(out=hc[:, n % 8, :], in0=h[:, n % 4, :], in1=bc_flat[:, ds(co, L)],
                                     op=ALU.mult).then_inc(hc_ready, 1)
                    for m, name in side_steps(POOL_AT, b, n):
                        (prep if name in PREP_STEPS else post)(m, name)

            po.wait_ge(dconst, 3)
            batch(0, FIRST)
            batch(0, SECOND)
            batch(1, FIRST)
            po.wait_ge(padded, 16)
            with po.Fori(1, NB - 1) as b:
                batch(b, SECOND)
                batch(b + 1, FIRST)
            batch(NB - 1, SECOND)
            for n in FIRST:
                for name in POOL_AT.get(n, ()):
                    post(NB - 1 if name in TURN else NB - 2, name)
            for i in range(6):
                post(NB - 1, f"g{i}")
            for j in range(2 * TT):
                if j == 0:
                    post(NB - 1, "g6")
                post(NB - 1, f"scatter{j}")

            def gather(i, c):
                po.wait_ge(row_list_in[c % 4], 16 * i + 16 * (c // 4 + 1))
                if c >= 4:
                    po.wait_ge(xt_full, 4 * i + c - 3)
                alone(po)
                po.indirect_dma_start(out=xb[:, c % 4, :], out_offset=None, in_=xn_d,
                                      in_offset=bass.IndirectOffsetOnAxis(ap=lst_rows[:, c % 4, 0:1], axis=0)
                                      ).then_inc(rows_in[c % 4], 16)

            def add(i, c):
                po.wait_ge(ob_ready, 4 * i + c + 1)
                if c >= 1:
                    po.wait_ge(added, 16 * (4 * i + c))
                alone(po)
                po.indirect_dma_start(out=acc_d, in_=ob[:, c % 2, :], in_offset=None, compute_op=ALU.add,
                                      out_offset=bass.IndirectOffsetOnAxis(ap=lst[:, c % 4, 0:1], axis=0)
                                      ).then_inc(added, 16)

            po.wait_ge(xn_out, 16 * (NB + 1))
            for c in range(4):
                gather(0, c)
            po.wait_ge(sums_out, 16 * (NB + 1))

            def step(i, c):
                if c + 4 < NBLK:
                    gather(i, c + 4)
                if c >= 1:
                    add(i, c - 1)

            blocks(po, step)
            add(0, NBLK - 1)
            po.memset(fin_half[:, :], -0.5).then_inc(rs_step, 1)
            for b in range(NB):
                po.wait_ge(stats, 2 * NB + b + 1)
                rstd_of(b * TT, (b + 1) * TT, fin_rstd, 2 * NB + b, (fin_mv, fin_ve, fin_half, fin_rs, fin_nb))

        @block.sync
        def _(sp):
            sp.dma_start(pk[:, :], A["pack"]).then_inc(packed, 16)
            sp.dma_start(xT[:, :, 0:L], A["xT"][:, :, 0:L]).then_inc(x_in, 16)
            sp.dma_start(wdt[:, :], A["wdt"]).then_inc(wdt_in, 16)
            sp.dma_start(sel_raw[:, :, :], A["sel"]).then_inc(sel_in, 16)
            sp.dma_start(tok[:, :], A["tok"]).then_inc(tok_in, 16)

            def moves(m):
                par = parity(sp, m)
                if not (isinstance(m, int) and m < 2):
                    sp.wait_ge(drive_in, NG * (m - 1))
                    alone(sp)
                for i in range(2):
                    sp.wait_ge(lo_ready, DT * m + i + 1)
                    alone(sp)
                    for side, src in ((0, hi[i]), (1, lo[i])):
                        for up_ in range(2):
                            to = slice(64 * (up_ ^ side), 64 * (up_ ^ side) + 64)
                            dst = hl[i][to, ds(par, 1), up_::2, :].rearrange("p a c l -> p (a c) l")
                            sp.dma_start(dst.bitcast(F32), src[64 * up_:64 * up_ + 64, :, :].bitcast(F32)
                                         ).then_inc(moved, 16)

            def rows_of(table, m):
                return table[ds(start(sp, m), L), :].rearrange("(t p) d -> p t d", p=P)

            def store(m, name):
                dst = rows_of((xn_d, acc_d)[name == "down1"], m)
                src = xn_of(m)[:, :, :]
                if name == "down1" and not (isinstance(m, int) and m == NB - 1):
                    src = gh[:, :, :].rearrange("p i (t d) -> p (i t) d", d=D)
                drain_of(sp, m, name)
                alone(sp)
                sp.dma_start(dst, src).then_inc((xn_out, sums_out)[name == "down1"], 16)

            for dt in range(DT):
                for i in range(2):
                    sp.wait_ge((first["lo"], lo_ready)[dt], i + 1)
                    for side, src in ((0, hi[i]), (1, lo[i])):
                        for up_ in range(2):
                            to = slice(64 * (up_ ^ side), 64 * (up_ ^ side) + 64)
                            sp.dma_start(hl[i][to, 0, 2 * dt + up_, :].bitcast(F32),
                                         src[64 * up_:64 * up_ + 64, dt, :].bitcast(F32)
                                         ).then_inc((first["moved"], moved)[dt], 16)
            for b in range(1, NB):
                sp.wait_ge(x_in, 16 * b)
                sp.dma_start(xT[:, :, b * L:(b + 1) * L], A["xT"][:, :, b * L:(b + 1) * L]).then_inc(x_in, 16)
            sp.dma_start(wg_raw[:, :, :, :], A["wgu"]).then_inc(shared_in, 16)
            sp.dma_start(list_d, A["list"]).then_inc(padded, 16)
            sp.wait_ge(dconst, 3)
            sp.dma_start(xn_d[T:T + P, :], xn4[:, 0, :]).then_inc(xn_out, 16)
            sp.dma_start(acc_d[T:T + P, :], xn4[:, 0, :]).then_inc(sums_out, 16)
            sp.dma_start(wd[:, :, :], A["wd"]).then_inc(down_in, 16)
            moves(1)
            with sp.Fori(1, NB - 1) as b:
                store(b - 1, "turn1")
                moves(b + 1)
                store(b - 1, "down1")
            store(NB - 2, "turn1")

            def load_piece(j):
                if j >= 3:
                    sp.wait_ge(lo_split, j - 2)
                sp.dma_start(w1_raw[:, j % 3, :], A["w1"][:, j // DT, j % DT, :]).then_inc(raw_in[j % 3], 16)

            def list_row(i, c):
                return sp.value_load(info[0:1, 1, ds(i * 4 + c, 1)], min_val=0, max_val=NLIST - P)

            def fetch_rows(i, c):
                row = list_row(i, c)
                if c >= 4:
                    sp.wait_ge(rows_in[c % 4], 16 * i + 16 * (c // 4))
                    alone(sp)
                sp.dma_start(lst_rows[:, c % 4, :], list_d[ds(row, P), :]).then_inc(row_list_in[c % 4], 16)

            def fetch(i, c):
                row = list_row(i, c)
                if c >= 4:
                    sp.wait_ge(added, 16 * (4 * i + c - 3))
                    alone(sp)
                sp.dma_start(lst[:, c % 4, :], list_d[ds(row, P), :]).then_inc(list_in[c % 4], 16)

            sp.wait_ge(y_taken, DT * NB)
            for j in range(3):
                load_piece(j)
            store(NB - 1, "turn1")
            load_piece(3)
            store(NB - 2, "down1")
            for j in range(4, 7):
                load_piece(j)
            sp.dma_start(w2[:, :, :, :], A["w2"]).then_inc(w2_in, 16)
            for j in range(7, 13):
                load_piece(j)
            sp.wait_ge(info_ready, 1)
            sp.wait_ge(scattered, 128 * NB)
            for c in range(4):
                fetch_rows(0, c)
                if c == 1:
                    load_piece(13)
            load_piece(14)
            store(NB - 1, "down1")
            load_piece(15)
            for c in range(4):
                fetch(0, c)
            fetch_rows(0, 4)

            def step(i, c):
                if c + 5 < NBLK:
                    fetch_rows(i, c + 5)
                if c >= 1 and c + 3 < NBLK:
                    fetch(i, c + 3)

            blocks(sp, step)
            sp.wait_ge(added, 16 * NBLK)
            for b in range(NB):
                sp.dma_start(fin[:, b, :, :],
                             acc_d[b * L:(b + 1) * L, :].rearrange("(t p) d -> p t d", p=P)).then_inc(fin_in[b], 16)
            for b in range(NB):
                if b < NB - 1:
                    sp.wait_ge(fin_ready, b + 1)
                else:
                    sp.wait_ge(last_ready, 1)
                sp.dma_start(out[b * L:(b + 1) * L, :].rearrange("(t p) d -> p t d", p=P),
                             fin_o[:, b, :, :]).then_inc(fin_out, 16)
            sp.wait_ge(fin_out, 16 * NB)


def kernel(**inputs):
    import concourse.bacc as _bacc
    from concourse.bass_utils import run_bass_kernel_spmd as _run

    x = np.asarray(inputs["L0_attn_x"])
    w_x, w_dt = np.asarray(inputs["L0_attn_W_x"]), np.asarray(inputs["L0_attn_W_dt"])

    def tiles(a):
        return np.ascontiguousarray(a.reshape(-1, P, a.shape[-1]).transpose(1, 0, 2))

    a_log = np.asarray(inputs["L0_attn_A_log"]).reshape(DT, 4, 4, GC, NS).transpose(4, 3, 0, 2, 1).reshape(P, NG)
    parts = {
        "wp": tiles(w_x.T).reshape(P, -1),
        "bdt": np.asarray(inputs["L0_attn_b_dt"]).reshape(DT, P).T,
        "dpar": np.asarray(inputs["L0_attn_D"]).reshape(DT, P).T,
        "alog": a_log,
        "rw": tiles(np.asarray(inputs["L0_ffn_router_w"])).reshape(P, -1),
    }
    row = np.arange(P)
    state, chan = row // GC, row % GC
    ysel = np.zeros((P, 4, 32), np.float32)
    for k in range(4):
        ysel[row, k, GC * k + chan] = 1
    sel = np.zeros((P, 8, P), np.float32)
    for j in range(8):
        sel[:, j, :] = (row[:, None] % 64) == (GC * j + chan)[None, :]
    bcsel = np.zeros((P, 2, P), np.float32)
    for k in range(2):
        for i in range(NS):
            bcsel[R + NS * k + i, k, state == i] = 1
    parts["bcsel"] = bcsel.reshape(P, -1)
    parts["ysel"] = ysel.reshape(P, -1)
    parts["ident"] = np.eye(P, dtype=np.float32)
    parts["lower"] = np.concatenate([np.triu(np.ones((P, P), np.float32), 1), np.ones((P, P), np.float32)], axis=1)
    for name, v in (("rev", E - np.arange(E)), ("region", REGION * np.arange(E)), ("expert", np.arange(E)),
                    ("block", np.arange(NBLK))):
        parts[name] = np.tile(v.astype(np.float32), (P, 1))
    slots = np.zeros((NLIST, 2), np.int32)
    slots[:, 0] = TRASH + np.arange(NLIST) % P
    arrays = {
        "pack": np.ascontiguousarray(np.concatenate([parts[n] for n, _ in PACK], axis=1)),
        "xT": tiles(x.reshape(T, D).T),
        "wdt": np.ascontiguousarray(w_dt.T),
        "sel": sel,
        "wgu": np.ascontiguousarray(np.stack([tiles(np.asarray(inputs["L0_ffn_w_gate"])),
                                              tiles(np.asarray(inputs["L0_ffn_w_up"]))], axis=1)),
        "wd": tiles(np.asarray(inputs["L0_ffn_w_down"])),
        "w1": np.ascontiguousarray(np.asarray(inputs["L0_ffn_w1"]).reshape(E, DT, P, 2 * INTER).transpose(2, 0, 1, 3)),
        "w2": np.ascontiguousarray(np.asarray(inputs["L0_ffn_w2"]).reshape(E, INTER // P, P, D).transpose(2, 0, 1, 3)),
        "tok": np.ascontiguousarray((row[:, None] + P * np.arange(T // P)[None, :]).astype(np.int32)),
        "list": slots,
    }
    nc = _bacc.Bacc("TRN2", target_bir_lowering=False, num_devices=1)
    args = {n: nc.dram_tensor(f"in_{n}", a.shape, mybir.dt.from_np(a.dtype), kind="ExternalInput").ap()
            for n, a in arrays.items()}
    out = nc.dram_tensor("out", (T, D), F32, kind="ExternalOutput").ap()
    program(nc, args, out)
    r = _run(nc, [{f"in_{n}": a for n, a in arrays.items()}], core_ids=[0])
    return r.results[0]["out"].reshape(x.shape)
```
